# Optimizing a Trainium2 kernel written in Bass

```python
import numpy as np
import jax
import jax.numpy as jnp

def _softmax(x, axis=-1):
    return jax.nn.softmax(x, axis=axis)

def _gelu(x):
    return jax.nn.gelu(x, approximate=True)

def _silu(x):
    return jax.nn.silu(x)

def _sigmoid(x):
    return jax.nn.sigmoid(x)

def _layernorm(x, axis=-1, eps=1e-05):
    m = jnp.mean(x, axis=axis, keepdims=True)
    v = jnp.var(x, axis=axis, keepdims=True)
    return (x - m) / jnp.sqrt(v + eps)

def _scatter_add(tgt, idx, src, axis=0):
    return tgt.at[idx].add(src)

def _segment_sum(src, seg, n):
    return jax.ops.segment_sum(src, seg, n)
kernel_name = 'mk_macaron_d1_jaxref_r8_a8038a'

def setup_inputs(seed: int=0):
    np.random.seed(seed)
    _w = jnp.asarray

    def _L0_attn_setup():
        import jax, jax.numpy as jnp
        import numpy as np
        D_MODEL = 256
        D_STATE = 64
        D_CONV = 4
        EXPAND = 2
        HEADDIM = 64
        NGROUPS = 1
        CHUNK = 64
        D_INNER = EXPAND * D_MODEL
        NHEADS = D_INNER // HEADDIM
        D_XBC = D_INNER + 2 * NGROUPS * D_STATE
        D_IN_PROJ = 2 * D_INNER + 2 * NGROUPS * D_STATE + NHEADS

        def segsum(x):
            T = x.shape[-1]
            mask_strict = jnp.tril(jnp.ones((T, T), bool), k=-1)
            mask_incl = jnp.tril(jnp.ones((T, T), bool), k=0)
            xe = jnp.where(mask_strict, x[..., :, None], 0.0)
            xseg = jnp.cumsum(xe, axis=-2)
            return jnp.where(mask_incl, xseg, -jnp.inf)

        def ssd_scan(X, A, Bm, Cm, block_len=CHUNK):
            b, seqlen, h, p = X.shape
            n = Bm.shape[-1]
            pad_len = (block_len - seqlen % block_len) % block_len
            if pad_len > 0:
                X = jnp.pad(X, ((0, 0), (0, pad_len), (0, 0), (0, 0)))
                A = jnp.pad(A, ((0, 0), (0, pad_len), (0, 0)))
                Bm = jnp.pad(Bm, ((0, 0), (0, pad_len), (0, 0), (0, 0)))
                Cm = jnp.pad(Cm, ((0, 0), (0, pad_len), (0, 0), (0, 0)))
            L = X.shape[1]
            c = L // block_len
            Xc = X.reshape(b, c, block_len, h, p)
            Ac = A.reshape(b, c, block_len, h).transpose(0, 3, 1, 2)
            Bc = Bm.reshape(b, c, block_len, h, n)
            Cc = Cm.reshape(b, c, block_len, h, n)
            A_cum = jnp.cumsum(Ac, axis=-1)
            Lmat = jnp.exp(segsum(Ac))
            CB = jnp.einsum('bclhn,bcshn->bhcls', Cc, Bc)
            Y_diag = jnp.einsum('bhcls,bcshp->bhclp', CB * Lmat, Xc)
            decay_states = jnp.exp(A_cum[..., -1:] - A_cum)
            states = jnp.einsum('bhcl,bclhn,bclhp->bhcpn', decay_states, Bc, Xc)
            init = jnp.zeros((b, h, 1, p, n), X.dtype)
            states = jnp.concatenate([init, states], axis=2)
            chunk_decay = jnp.pad(A_cum[..., -1], ((0, 0), (0, 0), (1, 0)))
            decay_chunk = jnp.exp(segsum(chunk_decay))
            new_states = jnp.einsum('bhzc,bhcpn->bhzpn', decay_chunk, states)[:, :, :-1]
            Y_off = jnp.einsum('bclhn,bhcpn,bhcl->bhclp', Cc, new_states, jnp.exp(A_cum))
            Y = (Y_diag + Y_off).transpose(0, 2, 3, 1, 4).reshape(b, L, h, p)
            if pad_len > 0:
                Y = Y[:, :seqlen]
            return Y

        def rmsnorm_grouped(x, w, ngroups, eps=1e-05):
            gs = x.shape[-1] // ngroups
            xg = x.reshape(*x.shape[:-1], ngroups, gs)
            xg = xg * jax.lax.rsqrt(jnp.mean(xg * xg, axis=-1, keepdims=True) + eps)
            return xg.reshape(x.shape) * w
        key = jax.random.key(seed)
        ks = jax.random.split(key, 8)
        B, L = (2, 512)
        u = jax.random.normal(ks[0], (B, L, D_MODEL), jnp.float32)
        W_in = jax.random.normal(ks[1], (D_IN_PROJ, D_MODEL), jnp.float32) * 0.02
        conv_w = jax.random.normal(ks[2], (D_XBC, D_CONV), jnp.float32) * 0.2
        conv_b = jnp.zeros((D_XBC,), jnp.float32)
        dt = jnp.exp(jax.random.uniform(ks[3], (NHEADS,)) * (np.log(0.1) - np.log(0.001)) + np.log(0.001))
        dt = jnp.clip(dt, 0.0001)
        dt_bias = dt + jnp.log(-jnp.expm1(-dt))
        A_log = jnp.log(jax.random.uniform(ks[4], (NHEADS,), minval=1.0, maxval=16.0))
        D_param = jnp.ones((NHEADS,), jnp.float32)
        norm_w = jnp.ones((D_INNER,), jnp.float32)
        W_out = jax.random.normal(ks[5], (D_MODEL, D_INNER), jnp.float32) * 0.02
        return dict(u=u, W_in=W_in, conv_w=conv_w, conv_b=conv_b, dt_bias=dt_bias, A_log=A_log, D_param=D_param, norm_w=norm_w, W_out=W_out)
    _L0_attn_in = _L0_attn_setup()

    def _L0_ffn_setup():
        import jax, jax.numpy as jnp
        import numpy as np
        B, S, D, I, E, K = (4, 128, 256, 128, 8, 2)
        key = jax.random.key(seed)
        ks = jax.random.split(key, 7)

        def w(k, shape, fan_in):
            return jax.random.normal(k, shape, dtype=jnp.float32) * fan_in ** (-0.5)
        return {'hidden_states': jax.random.normal(ks[0], (B, S, D), dtype=jnp.float32), 'router_w': w(ks[1], (D, E), D), 'gate_up_w': w(ks[2], (E, D, 2 * I), D), 'down_w': w(ks[3], (E, I, D), I), 'shared_gate_w': w(ks[4], (D, I), D), 'shared_up_w': w(ks[5], (D, I), D), 'shared_down_w': w(ks[6], (I, D), I)}
    _L0_ffn_in = _L0_ffn_setup()
    _d = {'L0_attn_u': _L0_attn_in['u'], 'L0_attn_W_in': _L0_attn_in['W_in'], 'L0_attn_conv_w': _L0_attn_in['conv_w'], 'L0_attn_conv_b': _L0_attn_in['conv_b'], 'L0_attn_dt_bias': _L0_attn_in['dt_bias'], 'L0_attn_A_log': _L0_attn_in['A_log'], 'L0_attn_D_param': _L0_attn_in['D_param'], 'L0_attn_norm_w': _L0_attn_in['norm_w'], 'L0_attn_W_out': _L0_attn_in['W_out'], 'L0_ffn_router_w': _L0_ffn_in['router_w'], 'L0_ffn_gate_up_w': _L0_ffn_in['gate_up_w'], 'L0_ffn_down_w': _L0_ffn_in['down_w'], 'L0_ffn_shared_gate_w': _L0_ffn_in['shared_gate_w'], 'L0_ffn_shared_up_w': _L0_ffn_in['shared_up_w'], 'L0_ffn_shared_down_w': _L0_ffn_in['shared_down_w']}
    _x0 = _d['L0_attn_u']
    _d['L0_attn_u'] = jax.random.normal(jax.random.fold_in(jax.random.key(seed), 1), (8, 256, 256), dtype=_x0.dtype)
    del _x0
    return _d

def reference(L0_attn_u, L0_attn_W_in, L0_attn_conv_w, L0_attn_conv_b, L0_attn_dt_bias, L0_attn_A_log, L0_attn_D_param, L0_attn_norm_w, L0_attn_W_out, L0_ffn_router_w, L0_ffn_gate_up_w, L0_ffn_down_w, L0_ffn_shared_gate_w, L0_ffn_shared_up_w, L0_ffn_shared_down_w):

    def _L0_attn_ref(u, W_in, conv_w, conv_b, dt_bias, A_log, D_param, norm_w, W_out):
        import jax, jax.numpy as jnp
        import numpy as np
        D_MODEL = 256
        D_STATE = 64
        D_CONV = 4
        EXPAND = 2
        HEADDIM = 64
        NGROUPS = 1
        CHUNK = 64
        D_INNER = EXPAND * D_MODEL
        NHEADS = D_INNER // HEADDIM
        D_XBC = D_INNER + 2 * NGROUPS * D_STATE
        D_IN_PROJ = 2 * D_INNER + 2 * NGROUPS * D_STATE + NHEADS

        def segsum(x):
            T = x.shape[-1]
            mask_strict = jnp.tril(jnp.ones((T, T), bool), k=-1)
            mask_incl = jnp.tril(jnp.ones((T, T), bool), k=0)
            xe = jnp.where(mask_strict, x[..., :, None], 0.0)
            xseg = jnp.cumsum(xe, axis=-2)
            return jnp.where(mask_incl, xseg, -jnp.inf)

        def ssd_scan(X, A, Bm, Cm, block_len=CHUNK):
            b, seqlen, h, p = X.shape
            n = Bm.shape[-1]
            pad_len = (block_len - seqlen % block_len) % block_len
            if pad_len > 0:
                X = jnp.pad(X, ((0, 0), (0, pad_len), (0, 0), (0, 0)))
                A = jnp.pad(A, ((0, 0), (0, pad_len), (0, 0)))
                Bm = jnp.pad(Bm, ((0, 0), (0, pad_len), (0, 0), (0, 0)))
                Cm = jnp.pad(Cm, ((0, 0), (0, pad_len), (0, 0), (0, 0)))
            L = X.shape[1]
            c = L // block_len
            Xc = X.reshape(b, c, block_len, h, p)
            Ac = A.reshape(b, c, block_len, h).transpose(0, 3, 1, 2)
            Bc = Bm.reshape(b, c, block_len, h, n)
            Cc = Cm.reshape(b, c, block_len, h, n)
            A_cum = jnp.cumsum(Ac, axis=-1)
            Lmat = jnp.exp(segsum(Ac))
            CB = jnp.einsum('bclhn,bcshn->bhcls', Cc, Bc)
            Y_diag = jnp.einsum('bhcls,bcshp->bhclp', CB * Lmat, Xc)
            decay_states = jnp.exp(A_cum[..., -1:] - A_cum)
            states = jnp.einsum('bhcl,bclhn,bclhp->bhcpn', decay_states, Bc, Xc)
            init = jnp.zeros((b, h, 1, p, n), X.dtype)
            states = jnp.concatenate([init, states], axis=2)
            chunk_decay = jnp.pad(A_cum[..., -1], ((0, 0), (0, 0), (1, 0)))
            decay_chunk = jnp.exp(segsum(chunk_decay))
            new_states = jnp.einsum('bhzc,bhcpn->bhzpn', decay_chunk, states)[:, :, :-1]
            Y_off = jnp.einsum('bclhn,bhcpn,bhcl->bhclp', Cc, new_states, jnp.exp(A_cum))
            Y = (Y_diag + Y_off).transpose(0, 2, 3, 1, 4).reshape(b, L, h, p)
            if pad_len > 0:
                Y = Y[:, :seqlen]
            return Y

        def rmsnorm_grouped(x, w, ngroups, eps=1e-05):
            gs = x.shape[-1] // ngroups
            xg = x.reshape(*x.shape[:-1], ngroups, gs)
            xg = xg * jax.lax.rsqrt(jnp.mean(xg * xg, axis=-1, keepdims=True) + eps)
            return xg.reshape(x.shape) * w
        B, L, _ = u.shape
        zxbcdt = u @ W_in.T
        z = zxbcdt[..., :D_INNER]
        xBC = zxbcdt[..., D_INNER:D_INNER + D_XBC]
        dt = zxbcdt[..., D_INNER + D_XBC:]
        xpad = jnp.pad(xBC, ((0, 0), (D_CONV - 1, 0), (0, 0)))
        conv = conv_b
        for k in range(D_CONV):
            conv = conv + conv_w[:, k] * xpad[:, k:k + L, :]
        xBC = jax.nn.silu(conv)
        x = xBC[..., :D_INNER].reshape(B, L, NHEADS, HEADDIM)
        B_ssm = xBC[..., D_INNER:D_INNER + NGROUPS * D_STATE].reshape(B, L, NGROUPS, D_STATE)
        C_ssm = xBC[..., D_INNER + NGROUPS * D_STATE:].reshape(B, L, NGROUPS, D_STATE)
        if NGROUPS < NHEADS:
            rep = NHEADS // NGROUPS
            B_ssm = jnp.repeat(B_ssm, rep, axis=2)
            C_ssm = jnp.repeat(C_ssm, rep, axis=2)
        dt = jax.nn.softplus(dt + dt_bias)
        A = -jnp.exp(A_log)
        y = ssd_scan(x * dt[..., None], A * dt, B_ssm, C_ssm, block_len=CHUNK)
        y = y + D_param[:, None] * x
        y = y.reshape(B, L, D_INNER)
        y = rmsnorm_grouped(y * jax.nn.silu(z), norm_w, NGROUPS)
        return y @ W_out.T

    def _L0_ffn_ref(hidden_states, router_w, gate_up_w, down_w, shared_gate_w, shared_up_w, shared_down_w):
        import jax, jax.numpy as jnp
        import numpy as np
        B, S, D, I, E, K = (4, 128, 256, 128, 8, 2)
        Bb, Ss, Dd = hidden_states.shape
        x = hidden_states.reshape(-1, Dd)
        T = x.shape[0]
        shared = jax.nn.silu(x @ shared_gate_w) * (x @ shared_up_w) @ shared_down_w
        logits = x @ router_w
        top_val, top_idx = jax.lax.top_k(logits, K)
        probs = jnp.zeros_like(logits).at[jnp.arange(T)[:, None], top_idx].set(jax.nn.sigmoid(top_val))
        xin = probs.T[:, :, None] * x[None]
        gu = jnp.einsum('etd,edf->etf', xin, gate_up_w)
        gate, up = jnp.split(gu, 2, axis=-1)
        h = jax.nn.silu(gate) * up
        expert_out = jnp.einsum('eti,eid->etd', h, down_w)
        combined = shared + expert_out.sum(axis=0)
        return combined.reshape(Bb, Ss, Dd)
    x = L0_attn_u
    x = x + 0.5 * _L0_ffn_ref(_layernorm(x, axis=-1), L0_ffn_router_w, L0_ffn_gate_up_w, L0_ffn_down_w, L0_ffn_shared_gate_w, L0_ffn_shared_up_w, L0_ffn_shared_down_w)
    x = x + _L0_attn_ref(_layernorm(x, axis=-1), L0_attn_W_in, L0_attn_conv_w, L0_attn_conv_b, L0_attn_dt_bias, L0_attn_A_log, L0_attn_D_param, L0_attn_norm_w, L0_attn_W_out)
    x = x + 0.5 * _L0_ffn_ref(_layernorm(x, axis=-1), L0_ffn_router_w, L0_ffn_gate_up_w, L0_ffn_down_w, L0_ffn_shared_gate_w, L0_ffn_shared_up_w, L0_ffn_shared_down_w)
    return x

_drawn_inputs = setup_inputs


def setup_inputs(seed=0):
    import zlib

    import numpy as np

    out = dict(_drawn_inputs(seed))
    spreads = {'L0_attn_conv_b': (0.0, 0.1), 'L0_attn_D_param': (1.0, 0.2), 'L0_attn_norm_w': (1.0, 0.2)}
    factors = {}
    for name, (base, spread) in spreads.items():
        noise = np.random.default_rng([zlib.crc32(name.encode()), seed]).standard_normal(out[name].shape)
        drawn = base * np.exp(spread * noise) if base else spread * noise
        out[name] = jnp.asarray(drawn.astype(out[name].dtype))
    for name, factor in factors.items():
        out[name] = (out[name] * factor).astype(out[name].dtype)
    return out
```

```python
from collections import namedtuple
from contextlib import ExitStack

import concourse.bass as bass
from concourse import mybir

F32 = mybir.dt.float32
F32R = mybir.dt.float32r
U32 = mybir.dt.uint32
ACT = mybir.ActivationFunctionType
ALU = mybir.AluOpType

P = 128
D = 256
KD = D // P
E = 8
I = 128
CG = 2 * I
H = 8
HD = 64
N = 64
DI = H * HD
KI = DI // P
TAPS = 4
SEQ = 256
G = 4
GT = G * P
NC = 5
EPS = 1e-5
ZC = D + H
CONV_ORDER = [4, 0, 1, 2, 3]
DT_OPS = 17
Z_AT = [[0], [1, 2], [3], []]
C_AT = [[], [0], [1, 2], [3, 4]]
ATANH = [1.0 / k for k in (15, 13, 11, 9, 7, 5, 3)]

SH = -1
ORDER = [0, 1, 2, 3, 4, 5, SH, 6, 7]
NSTEP = len(ORDER)
BEFORE = 3


def macaron_kernel(nc, u, wg_up, w_down, w_sh_gate, w_sh_up, w_sh_down, w_router, w_in_t, w_out_t,
                   conv_w, conv_b, dt_bias, a_log, d_param, norm_w, out):
    T = u.shape[0] // P
    NG = T // G
    LAST = BEFORE + NSTEP * T - 1
    EMPTY = (1, 2, BEFORE + NSTEP * (T - 1) + ORDER.index(SH))

    def real(q):
        return 0 <= q <= LAST and q not in EMPTY

    def count(q):
        if isinstance(q, int):
            return sum(real(k) for k in range(q + 1))
        return q - 1

    u_v = u.rearrange("(t p) d -> p t d", p=P)
    out_v = out.rearrange("(t p) d -> p t d", p=P)

    with ExitStack() as ctx:
        def sb(name, shape, dt=F32):
            return ctx.enter_context(nc.sbuf_tensor(name, shape, dt))

        def sem(name):
            return ctx.enter_context(nc.semaphore(name))

        bank = [ctx.enter_context(nc.psum_tensor(f"bank{i}", [P, 512], F32)) for i in range(8)]

        x = sb("x", [P, T, D])
        w1h, w1l = sb("w1h", [P, KD, CG + E + E * CG], F32R), sb("w1l", [P, KD, CG + E + E * CG], F32R)
        w2h, w2l = sb("w2h", [P, 1 + E, D], F32R), sb("w2l", [P, 1 + E, D], F32R)
        NIN = w_in_t.shape[1]
        wih, wil = sb("wih", [P, KD, NIN], F32R), sb("wil", [P, KD, NIN], F32R)
        woh, wol = sb("woh", [P, KI, D], F32R), sb("wol", [P, KI, D], F32R)
        RAW = CG + E
        raw1 = sb("raw1", [P, 2, KD, RAW])
        raw2 = sb("raw2", [P, 2, D])
        ident = sb("ident", [P, P])
        below = sb("below", [P, P])
        below_r = sb("below_r", [P, P], F32R)
        upto = sb("upto", [P, P])
        quarter = sb("quarter", [P, P])
        iota8 = sb("iota8", [P, E])
        half_neg = sb("half_neg", [P, G])
        cw, cb = sb("cw", [P, NC, TAPS]), sb("cb", [P, NC])
        nw = sb("nw", [P, KI])
        bias8, alog8, a8, d8 = sb("bias8", [P, H]), sb("alog8", [P, H]), sb("a8", [P, H]), sb("d8", [P, H])

        st6, mv = sb("st6", [P, 2, 6]), sb("mv", [P, 2, 2])
        ve, rstd = sb("ve", [P, 2]), sb("rstd", [P, 2])
        scratch = sb("scratch", [P, 4 * DI])
        turned_hi, turned_lo = sb("turned_hi", [P, KD * GT], F32R), sb("turned_lo", [P, KD * GT], F32R)
        xn = scratch[:, 0:2 * D].rearrange("p (s d) -> p s d", s=2)
        sil = scratch[:, 2 * D:2 * D + 3 * I].rearrange("p (s d) -> p s d", s=3)
        hid = scratch[:, 2 * D + 3 * I:2 * D + 6 * I].rearrange("p (s d) -> p s d", s=3)
        xTh, xTl = (a[:, 0:2 * D].rearrange("p (s k n) -> p s k n", s=2, k=KD) for a in (turned_hi, turned_lo))
        hTh, hTl = (a[:, 2 * D:2 * D + 3 * P].rearrange("p (s n) -> p s n", s=3) for a in (turned_hi, turned_lo))
        lg, top, topi, topf = sb("lg", [P, 2, E]), sb("top", [P, E]), sb("topi", [P, E], U32), sb("topf", [P, 2])
        one1, one2, th8, p2 = sb("one1", [P, E]), sb("one2", [P, E]), sb("th8", [P, E]), sb("p2", [P, E])
        prob = sb("prob", [P, 2, E])

        gst, gmv = sb("gst", [P, G, 6]), sb("gmv", [P, G, 2])
        gve, grstd = sb("gve", [P, G]), sb("grstd", [P, G])
        gxn = raw1[:].rearrange("p s k n -> p (s k n)")[:, 0:G * D].rearrange("p (g d) -> p g d", g=G)
        nTh, nTl = (a[:].rearrange("p (k n) -> p k n", k=KD) for a in (turned_hi, turned_lo))
        cin, cacc = sb("cin", [P, 2, GT]), sb("cacc", [P, 2, GT])
        cth = cin
        xc = sb("xc", [P, 2, KI, GT])
        BT, CT = sb("BT", [N, 2, GT]), sb("CT", [N, 2, GT])
        zs = sb("zs", [P, 2, G, DI])
        dtr = sb("dtr", [P, 2, G, H])
        dtv, dtu, dtn = sb("dtv", [P, G, H]), sb("dtu", [P, G, H]), sb("dtn", [P, G, H])
        dtd, dts, dts2, dtq = sb("dtd", [P, G, H]), sb("dts", [P, G, H]), sb("dts2", [P, G, H]), sb("dtq", [P, G, H])
        dt_half = sb("dt_half", [P, 2, G, H])
        dA = sb("dA", [P, 2, G, H])
        dAh, dAl = sb("dAh", [P, 2, G, H], F32R), sb("dAl", [P, 2, G, H], F32R)
        rh, rl = sb("rh", [P, H, P], F32R), sb("rl", [P, H, P], F32R)
        M = sb("M", [P, 2, H, P])
        edec = sb("edec", [P, 2, H])
        cbm = sb("cbm", [P, P])
        dtx = sb("dtx", [P, 2, DI])
        y, off, sq, dtxe = (scratch[:, i * DI:(i + 1) * DI] for i in range(4))
        xD = sb("xD", [P, 2, DI])
        Btok, state = sb("Btok", [P, N]), sb("state", [N, DI])
        yz, ss = sb("yz", [P, 2, DI]), sb("ss", [P, 2])
        vy, ry = sb("vy", [P, 2]), sb("ry", [P, 2])
        yTh, yTl = sb("yTh", [P, KI, P], F32R), sb("yTl", [P, KI, P], F32R)

        x_first = sem("x_first")
        x_in = [sem(f"x_in{i}") for i in range(NG)]
        par_in = sem("par_in")
        raw_in = [sem("raw_in0"), sem("raw_in1")]
        raw_hi, raw_lo = sem("raw_hi"), sem("raw_lo")
        const_done = sem("const_done")
        a8_done = sem("a8_done")
        stored = sem("stored")

        def family(prefix, names):
            names = names.split()
            return namedtuple("Signals", names)(*[sem(f"{prefix}_{n}") for n in names])

        FFN = [family(f"f{f}", "stats var rstd xn xT xhi xlo gate_up silu hidden hT hhi hlo down logits route tanh "
                      "prob added") for f in range(2)]
        S = family("s", "stats var rstd xn nT nhi nlo conv cin tap conv_tanh xc z z_tanh zs dt dt_raw dt_exp dA decay seg "
                   "misc xtok exp edec cbm M dtx xD btok dtxe y_mm carry state off off_mm y yoff yz sumsq vy ry yT yhi "
                   "ylo o added")
        conv_free = sem("conv_free")
        share_step = sem("share_step")

        chunks = []
        for e in range(1 + E):
            c0 = 0 if e == 0 else CG + E + (e - 1) * CG
            n = CG + E if e == 0 else CG
            chunks.append(("expert", e, c0, n))
        for c0 in range(0, NIN, RAW):
            chunks.append(("in", None, c0, min(RAW, NIN - c0)))
        for k in range(0, KI, 2):
            chunks.append(("out", None, k, D))

        def load_chunk(sp, c):
            kind, e, c0, n = chunks[c]
            r = c % 2
            if c >= 2:
                sp.wait_ge(raw_hi, c - 1)
                sp.wait_ge(raw_lo, c - 1)
            if kind == "expert":
                if e == 0:
                    for k in range(KD):
                        rows = slice(k * P, (k + 1) * P)
                        sp.dma_start(raw1[:, r, k, 0:I], w_sh_gate[rows, :]).then_inc(raw_in[r], 16)
                        sp.dma_start(raw1[:, r, k, I:CG], w_sh_up[rows, :]).then_inc(raw_in[r], 16)
                        sp.dma_start(raw1[:, r, k, CG:CG + E], w_router[rows, :]).then_inc(raw_in[r], 16)
                    sp.dma_start(raw2[:, r, :], w_sh_down).then_inc(raw_in[r], 16)
                else:
                    sp.dma_start(raw1[:, r, :, 0:CG], wg_up[e - 1].rearrange("(k p) f -> p k f", p=P)).then_inc(raw_in[r], 16)
                    sp.dma_start(raw2[:, r, :], w_down[e - 1]).then_inc(raw_in[r], 16)
            elif kind == "in":
                sp.dma_start(raw1[:, r, :, 0:n], w_in_t.rearrange("(k p) f -> p k f", p=P)[:, :, c0:c0 + n]).then_inc(raw_in[r], 16)
            else:
                sp.dma_start(raw1[:, r, :, 0:D], w_out_t.rearrange("(k p) f -> p k f", p=P)[:, c0:c0 + 2, :]).then_inc(raw_in[r], 16)

        def loads(c):
            kind, e, _, _ = chunks[c]
            return 1 if kind != "expert" else 7 if e == 0 else 2

        def raw_count(c):
            return 16 * sum(loads(k) for k in range(c % 2, c + 1, 2))

        def chunk_tiles(c):
            kind, e, c0, n = chunks[c]
            r = c % 2
            if kind == "expert":
                return [(raw1[:, r, :, 0:n], w1h[:, :, c0:c0 + n], w1l[:, :, c0:c0 + n]),
                        (raw2[:, r, :], w2h[:, e, :], w2l[:, e, :])]
            if kind == "in":
                return [(raw1[:, r, :, 0:n], wih[:, :, c0:c0 + n], wil[:, :, c0:c0 + n])]
            return [(raw1[:, r, :, 0:D], woh[:, c0:c0 + 2, :], wol[:, c0:c0 + 2, :])]

        def as_f32(ap):
            return ap.bitcast(F32)

        block = ctx.enter_context(nc.Block())

        @block.sync
        def _(sp):
            sp.dma_start(x[:, 0:1, :], u_v[:, 0:1, :]).then_inc(x_first, 16)
            load_chunk(sp, 0)
            sp.dma_start(x[:, 1:G, :], u_v[:, 1:G, :]).then_inc(x_in[0], 16)
            load_chunk(sp, 1)
            for i in range(1, NG):
                sp.dma_start(x[:, G * i:G * i + G, :], u_v[:, G * i:G * i + G, :]).then_inc(x_in[i], 16)
            for c in range(2, len(chunks)):
                load_chunk(sp, c)
            with sp.Fori(0, T) as t:
                sp.wait_ge(FFN[1].added, t + 1)
                sp.dma_start(out_v[:, bass.ds(t, 1), :], x[:, bass.ds(t, 1), :]).then_inc(stored, 16)
            sp.wait_ge(stored, 16 * T)

        @block.gpsimd
        def _(pool):
            pool.memset(ident[:], 0.0).then_inc(const_done, 1)
            pool.memset(upto[:], 0.0).then_inc(const_done, 1)
            pool.memset(quarter[:], 0.0).then_inc(const_done, 1)
            pool.memset(below[:], 0.0).then_inc(const_done, 1)
            pool.memset(half_neg[:], -0.5).then_inc(const_done, 1)
            pool.wait_ge(const_done, 5)
            pool.affine_select(out=ident[:], in_=ident[:], compare_op=ALU.not_equal, fill=1.0, base=0,
                               pattern=[[-1, P]], channel_multiplier=1).then_inc(const_done, 1)
            pool.affine_select(out=upto[:], in_=upto[:], compare_op=ALU.is_gt, fill=1.0, base=0,
                               pattern=[[-1, P]], channel_multiplier=1).then_inc(const_done, 1)
            pool.affine_select(out=quarter[:], in_=quarter[:], compare_op=ALU.is_gt, fill=0.25, base=0,
                               pattern=[[-1, P]], channel_multiplier=1).then_inc(const_done, 1)
            pool.affine_select(out=below[:], in_=below[:], compare_op=ALU.is_ge, fill=1.0, base=0,
                               pattern=[[1, P]], channel_multiplier=-1).then_inc(const_done, 1)
            pool.iota(iota8[:], pattern=[[1, E]], base=0, channel_multiplier=0,
                      allow_small_or_imprecise_dtypes=True).then_inc(const_done, 1)

            def root(F, t, s):
                pool.wait_ge(F.var, t + 1)
                pool.tensor_tensor(rstd[:, s:s + 1], ve[:, s:s + 1], half_neg[:, 0:1], ALU.pow).then_inc(F.rstd, 1)

            def ffn(F):
                with pool.Fori(0, T // 2) as i:
                    for s in range(2):
                        root(F, 2 * i + s, s)

            ffn(FFN[0])

            def group_root(g):
                pool.wait_ge(S.stats, 2 * G * (g + 1))
                pool.tensor_scalar(gve[:], gmv[:, :, 1], EPS, None, ALU.add).then_inc(S.var, 1)
                pool.wait_ge(S.var, g + 1)
                pool.tensor_tensor(grstd[:], gve[:], half_neg[:], ALU.pow).then_inc(S.rstd, 1)

            def decay(t):
                g, j = divmod(t, G)
                pool.wait_ge(S.dA, 2 * (g + 1))
                if t:
                    pool.wait_ge(S.seg, t)
                for r, a in ((rh, dAh), (rl, dAl)):
                    pool.tensor_tensor(r[:], upto[:].unsqueeze(1).broadcast_to([P, H, P]),
                                       as_f32(a[:, g % 2, j, :]).unsqueeze(2).broadcast_to([P, H, P]),
                                       ALU.mult).then_inc(S.decay, 1)

            def gate(t):
                g, j = divmod(t, G)
                pool.wait_ge(S.y, t + 1)
                if t % 2:
                    pool.wait_ge(S.off, t // 2 + 1)
                    pool.tensor_tensor(y, y, off, ALU.add).then_inc(S.yoff, 1)
                    pool.wait_ge(S.yoff, t // 2 + 1)
                if t >= 2:
                    pool.wait_ge(S.yT, t - 1)
                    pool.wait_ge(S.sumsq, t - 1)
                pool.tensor_tensor(yz[:, t % 2, :], y, zs[:, g % 2, j, :], ALU.mult).then_inc(S.yz, 1)

            def norm_root(t):
                pool.wait_ge(S.sumsq, t + 1)
                pool.tensor_scalar(vy[:, t % 2:t % 2 + 1], ss[:, t % 2:t % 2 + 1], 1.0 / (4 * DI), EPS,
                                   ALU.mult, ALU.add).then_inc(S.vy, 1)
                pool.wait_ge(S.vy, t + 1)
                if t >= 2:
                    pool.wait_ge(S.added, t - 1)
                pool.tensor_tensor(ry[:, t % 2:t % 2 + 1], vy[:, t % 2:t % 2 + 1], half_neg[:, 0:1],
                                   ALU.pow).then_inc(S.ry, 1)

            def scaled_inputs(t):
                pool.wait_ge(S.dtx, t + 1)
                pool.wait_ge(S.edec, t + 1)
                if t >= 2:
                    pool.wait_ge(S.carry, t // 2)
                pool.tensor_tensor(dtxe.rearrange("p (h d) -> p h d", h=H),
                                   dtx[:, t % 2, :].rearrange("p (h d) -> p h d", h=H),
                                   edec[:, t % 2, :].unsqueeze(2).broadcast_to([P, H, HD]),
                                   ALU.mult).then_inc(S.dtxe, 1)

            group_root(0)
            decay(0)
            for t in range(T + 2):
                if t < T and t % 2 == 0:
                    scaled_inputs(t)
                if t < T and t % G == 0 and t // G + 1 < NG:
                    group_root(t // G + 1)
                if 1 <= t <= T:
                    gate(t - 1)
                if t + 1 < T:
                    decay(t + 1)
                if 1 <= t <= T:
                    norm_root(t - 1)

            ffn(FFN[1])

        @block.scalar
        def _(act):
            params = [(cw[:], conv_w), (cb[:], conv_b), (nw[:], norm_w),
                      (bias8[:], dt_bias.partition_broadcast(P)), (alog8[:], a_log.partition_broadcast(P)),
                      (d8[:], d_param.partition_broadcast(P))]
            for to, of in params:
                act.dma_start(to, of).then_inc(par_in, 16)

            def split_hi(c):
                act.wait_ge(raw_in[c % 2], raw_count(c))
                kind, _, k, _ = chunks[c]
                parts = chunk_tiles(c)
                if kind == "out":
                    act.wait_ge(a8_done, 2)
                    for b in range(2):
                        ins = act.activation(raw1[:, c % 2, b, 0:D], raw1[:, c % 2, b, 0:D], ACT.Copy,
                                             scale=nw[:, k + b:k + b + 1])
                    ins.then_inc(a8_done, 1)
                    act.wait_ge(a8_done, 3 + k // 2)
                for n, (raw, hi, lo) in enumerate(parts):
                    ins = act.activation(hi, raw, ACT.Copy)
                ins.then_inc(raw_hi, 1)

            def x_hi(F, t, s):
                act.wait_ge(F.xT, t + 1)
                act.activation(xTh[:, s], bank[7][:, 0:D].rearrange("p (k n) -> p k n", k=KD),
                               ACT.Copy).then_inc(F.xhi, 1)

            def silu(F, q, r, t, s, e):
                act.wait_ge(F.gate_up, count(q))
                if not isinstance(q, int) or q >= 3:
                    act.wait_ge(F.hidden, count(q - 3))
                if e == SH:
                    act.activation(sil[:, r % 3, :], bank[r % 3][:, 0:I], ACT.Silu).then_inc(F.silu, 1)
                else:
                    act.wait_ge(F.prob, t + 1)
                    act.activation(sil[:, r % 3, :], bank[r % 3][:, 0:I], ACT.Silu,
                                   scale=prob[:, s, e:e + 1]).then_inc(F.silu, 1)

            def h_hi(F, q, r):
                act.wait_ge(F.hT, count(q))
                if not isinstance(q, int) or q >= 3:
                    act.wait_ge(F.down, count(q - 3))
                act.activation(hTh[:, r % 3, :], bank[3 + r % 2][:, 0:P], ACT.Copy).then_inc(F.hhi, 1)

            def tanh_logits(F, t, s):
                act.wait_ge(F.logits, t + 1)
                act.activation(th8[:], lg[:, s, :], ACT.Tanh, scale=0.5).then_inc(F.tanh, 1)

            def ffn(F, first):
                if first:
                    split_hi(0)
                x_hi(F, 0, 0)
                silu(F, 0, 0, 0, 0, SH)
                tanh_logits(F, 0, 0)
                h_hi(F, 0, 0)

                def tile(t, s, split):
                    q0 = t * NSTEP + BEFORE
                    for j, e in enumerate(ORDER):
                        q, r = q0 + j, s * NSTEP + BEFORE + j
                        last = isinstance(t, int) and t == T - 1
                        if split and e != SH:
                            split_hi(1 + e)
                        if not (last and e == SH):
                            silu(F, q, r, t, s, e)
                        if not isinstance(q, int) or real(q - 2):
                            h_hi(F, q - 2, r - 2)
                        if j == 4 and not last:
                            x_hi(F, t + 1, 1 - s)
                        if e == SH and not last:
                            tanh_logits(F, t + 1, 1 - s)

                for s in range(2):
                    tile(s, s, first and s == 0)
                if first:
                    for c in range(1 + E, len(chunks)):
                        split_hi(c)
                with act.Fori(1, T // 2 - 1) as i:
                    for s in range(2):
                        tile(2 * i + s, s, False)
                for s in range(2):
                    tile(T - 2 + s, s, False)
                for q in (LAST - 1, LAST):
                    h_hi(F, q, q - NSTEP * (T - 2))

            act.wait_ge(par_in, 16 * len(params))
            act.activation(a8[:], alog8[:], ACT.Exp).then_inc(a8_done, 1)
            act.activation(nw[:], nw[:], ACT.Copy, scale=0.5).then_inc(a8_done, 1)
            ffn(FFN[0], True)

            def n_hi(g, pair):
                act.wait_ge(S.nT, 2 * g + pair + 1)
                if g:
                    act.wait_ge(S.conv, 5 * g)
                    act.wait_ge(S.z, 8 * g)
                src = bank[7 - 2 * pair][:].rearrange("p (k n) -> p k n", k=KD)
                act.activation(nTh[:, :, pair * 2 * P:(pair + 1) * 2 * P], src, ACT.Copy).then_inc(S.nhi, 1)

            def conv_in(i):
                c = CONV_ORDER[i % NC]
                act.wait_ge(S.conv, i + 1)
                if i >= 2:
                    act.wait_ge(S.xc, i - 1)
                act.activation(cin[:, i % 2, :], bank[5][:], ACT.Copy).then_inc(S.cin, 1)
                act.activation(cacc[:, i % 2, :], bank[5][:], ACT.Identity, scale=cw[:, c, TAPS - 1:TAPS],
                               bias=cb[:, c:c + 1]).then_inc(conv_free, 1)

            def conv_tanh(i):
                act.wait_ge(S.tap, (TAPS - 1) * (i + 1))
                act.activation(cth[:, i % 2, :], cacc[:, i % 2, :], ACT.Tanh, scale=0.5).then_inc(S.conv_tanh, 1)

            def z_tanh(i):
                for half in range(2):
                    n = 2 * i + half
                    act.wait_ge(S.z, n + 1)
                    g, j = divmod(i, G)
                    if j == 0 and g >= 2:
                        act.wait_ge(S.yz, G * (g - 1))
                    act.activation(zs[:, g % 2, j, half * D:(half + 1) * D], bank[5 + half][:, 0:D], ACT.Tanh,
                                   scale=0.5).then_inc(S.z_tanh, 1)

            def dt_exp(g):
                act.wait_ge(S.dt, DT_OPS * g + 2)
                act.activation(dtu[:], dtn[:], ACT.Exp).then_inc(S.dt_exp, 1)

            def decays(t):
                act.wait_ge(S.seg, t + 1)
                if t >= 2:
                    act.wait_ge(S.y_mm, t - 1)
                for half in range(2):
                    act.activation(M[:, t % 2, half * 4:half * 4 + 4, :], bank[half][:].rearrange("p (h n) -> p h n", h=4),
                                   ACT.Exp).then_inc(S.exp, 1)
                act.wait_ge(S.misc, t + 1)
                act.activation(edec[:, t % 2, :], bank[3][:, P:P + H], ACT.Exp).then_inc(S.edec, 1)

            def carried(t):
                act.wait_ge(S.carry, t // 2 + 1)
                act.activation(state[:], bank[7][0:N, :], ACT.Copy, scale=0.25).then_inc(S.state, 1)

            def square(t):
                act.wait_ge(S.yz, t + 1)
                if t >= 2:
                    act.wait_ge(S.vy, t - 1)
                if t:
                    act.wait_ge(S.sumsq, t)
                act.activation(sq, yz[:, t % 2, :], ACT.Square, accum_out=ss[:, t % 2:t % 2 + 1]).then_inc(S.sumsq, 1)

            def y_hi(t):
                act.wait_ge(S.yT, t + 1)
                if t:
                    act.wait_ge(S.o, t)
                act.activation(yTh[:], bank[6][:].rearrange("p (k n) -> p k n", k=KI), ACT.Copy).then_inc(S.yhi, 1)

            n_hi(0, 0)
            n_hi(0, 1)
            for j in range(G):
                z_tanh(j)
            dt_exp(0)
            for k in range(NC):
                conv_in(k)
                if k:
                    conv_tanh(k - 1)
            conv_tanh(NC - 1)
            for t in range(T + 2):
                g, j = divmod(t, G)
                more = g + 1 < NG
                zs_, cs_ = (Z_AT[j], C_AT[j]) if more else ([], [])
                if t < T:
                    decays(t)
                if t >= 2:
                    y_hi(t - 2)
                for n, k in enumerate(cs_):
                    conv_in(NC * (g + 1) + k)
                    if n == 0 and t % 2 and t <= T:
                        carried(t - 1)
                if not cs_ and t % 2 and t <= T:
                    carried(t - 1)
                for k in cs_:
                    conv_tanh(NC * (g + 1) + k)
                if j == 0 and more:
                    n_hi(g + 1, 0)
                    n_hi(g + 1, 1)
                for k in zs_:
                    z_tanh(G * (g + 1) + k)
                if more and j == 2:
                    dt_exp(g + 1)
                if 1 <= t <= T:
                    square(t - 1)

            ffn(FFN[1], False)

        @block.vector
        def _(dve):
            def split_lo(c):
                dve.wait_ge(raw_hi, c + 1)
                for raw, hi, lo in chunk_tiles(c):
                    ins = dve.tensor_tensor(lo, raw, as_f32(hi), ALU.subtract)
                ins.then_inc(raw_lo, 1)

            def stats(F, t, s, ready):
                ready(t)
                dve.bn_stats(st6[:, s, :], x[:, bass.ds(t, 1), :].squeeze(1) if not isinstance(t, int) else x[:, t, :]).then_inc(F.stats, 1)
                dve.drain()
                dve.bn_aggr(mv[:, s, :], st6[:, s, :]).then_inc(F.stats, 1)
                dve.wait_ge(F.stats, 2 * t + 2)
                dve.tensor_scalar(ve[:, s:s + 1], mv[:, s, 1:2], EPS, None, ALU.add).then_inc(F.var, 1)

            def normal(F, t, s):
                dve.wait_ge(F.rstd, t + 1)
                if not isinstance(t, int) or t >= 2:
                    dve.wait_ge(F.xT, t - 1)
                src = x[:, bass.ds(t, 1), :].squeeze(1) if not isinstance(t, int) else x[:, t, :]
                dve.tensor_scalar(xn[:, s, :], src, mv[:, s, 0:1], rstd[:, s:s + 1], ALU.subtract,
                                  ALU.mult).then_inc(F.xn, 1)

            def x_lo(F, t, s):
                dve.wait_ge(F.xhi, t + 1)
                dve.tensor_tensor(xTl[:, s], bank[7][:, 0:D].rearrange("p (k n) -> p k n", k=KD), as_f32(xTh[:, s]),
                                  ALU.subtract).then_inc(F.xlo, 1)

            def hidden(F, q, r, s, e):
                dve.wait_ge(F.silu, count(q))
                if not isinstance(q, int) or q >= 3:
                    dve.wait_ge(F.hT, count(q - 3))
                if e == SH:
                    dve.tensor_copy(lg[:, s, :], bank[r % 3][:, CG:CG + E]).then_inc(F.logits, 1)
                    dve.tensor_tensor(hid[:, r % 3, :], bank[r % 3][:, I:CG], sil[:, r % 3, :],
                                      ALU.mult).then_inc(F.hidden, 1)
                else:
                    dve.scalar_tensor_tensor(out=hid[:, r % 3, :], in0=bank[r % 3][:, I:CG], scalar=prob[:, s, e:e + 1],
                                             in1=sil[:, r % 3, :], op0=ALU.mult, op1=ALU.mult).then_inc(F.hidden, 1)

            def h_lo(F, q, r):
                dve.wait_ge(F.hhi, count(q))
                dve.tensor_tensor(hTl[:, r % 3, :], bank[3 + r % 2][:, 0:P], as_f32(hTh[:, r % 3, :]),
                                  ALU.subtract).then_inc(F.hlo, 1)

            def route(F, t, s):
                n = 5 * t
                dve.drain()
                dve.max(top[:], lg[:, s, :]).then_inc(F.route, 1)
                dve.drain()
                dve.max_index(topi[:], top[:], lg[:, s, :]).then_inc(F.route, 1)
                dve.wait_ge(F.route, n + 2)
                dve.tensor_copy(topf[:], topi[:, 0:2]).then_inc(F.route, 1)
                dve.wait_ge(F.route, n + 3)
                dve.tensor_scalar(one1[:], iota8[:], topf[:, 0:1], None, ALU.is_equal).then_inc(F.route, 1)
                dve.wait_ge(F.route, n + 4)
                dve.scalar_tensor_tensor(out=one2[:], in0=iota8[:], scalar=topf[:, 1:2], in1=one1[:],
                                         op0=ALU.is_equal, op1=ALU.add).then_inc(F.route, 1)

            def shares(F, t, s):
                dve.wait_ge(F.tanh, t + 1)
                dve.wait_ge(F.route, 5 * t + 5)
                dve.scalar_tensor_tensor(out=p2[:], in0=th8[:], scalar=1.0, in1=one2[:], op0=ALU.add,
                                         op1=ALU.mult).then_inc(share_step, 1)
                dve.wait_ge(share_step, t + 1 + (0 if F is FFN[0] else T))
                dve.tensor_scalar(prob[:, s, :], p2[:], 0.5, None, ALU.mult).then_inc(F.prob, 1)

            def add_out(F, t, s):
                q = (t + 1) * NSTEP + BEFORE - 1
                dve.wait_ge(F.down, count(q))
                to = x[:, t, :] if isinstance(t, int) else x[:, bass.ds(t, 1), :].squeeze(1)
                dve.scalar_tensor_tensor(out=to, in0=bank[5 + s][:, 0:D], scalar=0.5, in1=to, op0=ALU.mult,
                                         op1=ALU.add).then_inc(F.added, 1)

            def ffn(F, first, ready):
                stats(F, 0, 0, ready)
                if first:
                    split_lo(0)
                normal(F, 0, 0)
                x_lo(F, 0, 0)
                hidden(F, 0, 0, 0, SH)
                route(F, 0, 0)
                h_lo(F, 0, 0)
                shares(F, 0, 0)

                def tile(t, s, split):
                    q0 = t * NSTEP + BEFORE
                    last = isinstance(t, int) and t == T - 1
                    for j, e in enumerate(ORDER):
                        q, r = q0 + j, s * NSTEP + BEFORE + j
                        if split and e != SH:
                            split_lo(1 + e)
                        if j == 0 and not last:
                            stats(F, t + 1, 1 - s, ready)
                        if not (last and e == SH):
                            hidden(F, q, r, s if e != SH else 1 - s, e)
                        if not isinstance(q, int) or real(q - 2):
                            h_lo(F, q - 2, r - 2)
                        if j == 2 and not last:
                            normal(F, t + 1, 1 - s)
                        if j == 3 and not (isinstance(t, int) and t == 0):
                            add_out(F, t - 1, 1 - s)
                        if j == 4 and not last:
                            x_lo(F, t + 1, 1 - s)
                        if e == SH and not last:
                            route(F, t + 1, 1 - s)
                        if j == 7 and not last:
                            shares(F, t + 1, 1 - s)

                for s in range(2):
                    tile(s, s, first and s == 0)
                if first:
                    for c in range(1 + E, len(chunks)):
                        split_lo(c)
                with dve.Fori(1, T // 2 - 1) as i:
                    for s in range(2):
                        tile(2 * i + s, s, False)
                for s in range(2):
                    tile(T - 2 + s, s, False)
                for q in (LAST - 1, LAST):
                    h_lo(F, q, q - NSTEP * (T - 2))
                add_out(F, T - 1, 1)

            dve.wait_ge(const_done, 10)
            dve.tensor_copy(below_r[:], below[:]).then_inc(const_done, 1)
            dve.wait_ge(a8_done, 1)
            dve.wait_ge(par_in, 96)
            dve.tensor_scalar(a8[:], a8[:], -1.0, None, ALU.mult).then_inc(const_done, 1)
            dve.tensor_scalar(d8[:], d8[:], 0.5, None, ALU.mult).then_inc(const_done, 1)

            def first_ready(t):
                if isinstance(t, int) and t == 0:
                    dve.wait_ge(x_first, 16)
                if isinstance(t, int) and t == 1:
                    dve.wait_ge(x_in[0], 16)
                if isinstance(t, int) and t == 2:
                    for i in range(1, NG):
                        dve.wait_ge(x_in[i], 16)

            ffn(FFN[0], True, first_ready)

            def g_stats(g):
                for j in range(G):
                    dve.wait_ge(FFN[0].added, G * g + j + 1)
                    if g:
                        dve.wait_ge(S.xn, G * g)
                    dve.bn_stats(gst[:, j, :], x[:, G * g + j, :]).then_inc(S.stats, 1)
                for j in range(G):
                    dve.wait_ge(S.stats, 2 * G * g + G)
                    dve.bn_aggr(gmv[:, j, :], gst[:, j, :]).then_inc(S.stats, 1)

            def g_normal(g):
                dve.wait_ge(S.rstd, g + 1)
                if g:
                    dve.wait_ge(S.nT, 2 * g)
                for j in range(G):
                    dve.tensor_scalar(gxn[:, j, :], x[:, G * g + j, :], gmv[:, j, 0:1], grstd[:, j:j + 1],
                                      ALU.subtract, ALU.mult).then_inc(S.xn, 1)

            def n_lo(g, pair):
                dve.wait_ge(S.nhi, 2 * g + pair + 1)
                cols = slice(pair * 2 * P, (pair + 1) * 2 * P)
                dve.tensor_tensor(nTl[:, :, cols], bank[7 - 2 * pair][:].rearrange("p (k n) -> p k n", k=KD),
                                  as_f32(nTh[:, :, cols]), ALU.subtract).then_inc(S.nlo, 1)

            def z_silu(i):
                g, j = divmod(i, G)
                for half in range(2):
                    dve.wait_ge(S.z_tanh, 2 * i + half + 1)
                    if half == 0:
                        dve.tensor_copy(dtr[:, g % 2, j, :], bank[5][:, D:ZC]).then_inc(S.dt_raw, 1)
                    z = zs[:, g % 2, j, half * D:(half + 1) * D]
                    dve.scalar_tensor_tensor(out=z, in0=z, scalar=1.0,
                                             in1=bank[5 + half][:, 0:D], op0=ALU.add, op1=ALU.mult).then_inc(S.zs, 1)

            def dt_chain(g, part):
                n = DT_OPS * g

                def step(k, ins):
                    ins.then_inc(S.dt, 1)
                    dve.wait_ge(S.dt, n + k)

                gp = g % 2
                if part == 0:
                    dve.wait_ge(S.dt_raw, G * (g + 1))
                    if g:
                        dve.wait_ge(S.dt, n)
                    step(1, dve.tensor_tensor(dtv[:], dtr[:, gp], bias8[:].unsqueeze(1).broadcast_to([P, G, H]), ALU.add))
                    step(2, dve.scalar_tensor_tensor(out=dtn[:], in0=dtv[:], scalar=-1.0, in1=dtv[:], op0=ALU.mult, op1=ALU.min))
                    return
                dve.wait_ge(S.dt_exp, g + 1)
                step(3, dve.tensor_scalar(dtd[:], dtu[:], 2.0, None, ALU.add))
                step(4, dve.reciprocal(dtd[:], dtd[:]))
                step(5, dve.tensor_tensor(dts[:], dtu[:], dtd[:], ALU.mult))
                step(6, dve.tensor_tensor(dts2[:], dts[:], dts[:], ALU.mult))
                step(7, dve.tensor_scalar(dtq[:], dts2[:], ATANH[0], None, ALU.mult))
                k = 8
                for c in ATANH[1:]:
                    step(k, dve.scalar_tensor_tensor(out=dtq[:], in0=dtq[:], scalar=c, in1=dts2[:], op0=ALU.add, op1=ALU.mult))
                    k += 1
                step(k, dve.scalar_tensor_tensor(out=dtq[:], in0=dtq[:], scalar=1.0, in1=dts[:], op0=ALU.add, op1=ALU.mult))
                step(k + 1, dve.tensor_scalar(dtv[:], dtv[:], 0.0, 0.5, ALU.max, ALU.mult))
                if g >= 2:
                    dve.wait_ge(S.misc, G * (g - 1))
                step(k + 2, dve.tensor_tensor(dt_half[:, gp], dtq[:], dtv[:], ALU.add))
                assert k + 3 == DT_OPS
                step(k + 3, dve.scalar_tensor_tensor(out=dA[:, gp], in0=dt_half[:, gp], scalar=2.0,
                                                     in1=a8[:].unsqueeze(1).broadcast_to([P, G, H]), op0=ALU.mult, op1=ALU.mult))
                dve.tensor_copy(dAh[:, gp], dA[:, gp]).then_inc(S.dA, 1)
                dve.wait_ge(S.dA, 2 * g + 1)
                dve.tensor_tensor(dAl[:, gp], dA[:, gp], as_f32(dAh[:, gp]), ALU.subtract).then_inc(S.dA, 1)

            def conv(i):
                g, k = divmod(i, NC)
                c = CONV_ORDER[k]
                dve.wait_ge(conv_free, i + 1)
                a = cacc[:, i % 2, :].rearrange("p (b l) -> p b l", l=SEQ)
                r = cin[:, i % 2, :].rearrange("p (b l) -> p b l", l=SEQ)
                for s in range(1, TAPS):
                    n = (TAPS - 1) * i + s
                    if s > 1:
                        dve.wait_ge(S.tap, n - 1)
                    dve.scalar_tensor_tensor(out=a[:, :, s:SEQ], in0=r[:, :, 0:SEQ - s], scalar=cw[:, c, TAPS - 1 - s:TAPS - s],
                                             in1=a[:, :, s:SEQ], op0=ALU.mult, op1=ALU.add).then_inc(S.tap, 1)

            def conv_silu(i):
                g, k = divmod(i, NC)
                c = CONV_ORDER[k]
                dve.wait_ge(S.conv_tanh, i + 1)
                if g >= 2 and k == 0:
                    dve.wait_ge(S.xtok, G * (g - 1))
                    dve.wait_ge(S.carry, G * (g - 1) // 2)
                    dve.wait_ge(S.off_mm, G * (g - 1) // 2)
                if c < KI:
                    dve.scalar_tensor_tensor(out=xc[:, g % 2, c, :], in0=cth[:, i % 2, :], scalar=1.0, in1=cacc[:, i % 2, :],
                                             op0=ALU.add, op1=ALU.mult).then_inc(S.xc, 1)
                    return
                dve.scalar_tensor_tensor(out=BT[:, g % 2, :], in0=cth[0:N, i % 2, :], scalar=1.0, in1=cacc[0:N, i % 2, :],
                                         op0=ALU.add, op1=ALU.mult)
                dve.scalar_tensor_tensor(out=CT[:, g % 2, :], in0=cth[N:P, i % 2, :], scalar=1.0, in1=cacc[N:P, i % 2, :],
                                         op0=ALU.add, op1=ALU.mult).then_inc(S.xc, 1)

            def heads(ap):
                return ap.rearrange("p (h d) -> p h d", h=H)

            def mix(t):
                g, j = divmod(t, G)
                dve.wait_ge(S.edec, t + 1)
                if t:
                    dve.wait_ge(S.M, 2 * t)
                dve.tensor_tensor(cbm[:], bank[3][:, 0:P], quarter[:], ALU.mult).then_inc(S.cbm, 1)
                if t % 2 == 0:
                    if t:
                        dve.wait_ge(S.carry, t // 2)
                    dve.tensor_copy(Btok[:], bank[3][:, 256:256 + N]).then_inc(S.btok, 1)
                dve.wait_ge(S.cbm, t + 1)
                if t >= 2:
                    dve.wait_ge(S.y_mm, t - 1)
                for half in range(2):
                    dve.wait_ge(S.exp, 2 * t + half + 1)
                    hs = slice(4 * half, 4 * half + 4)
                    dve.tensor_tensor(M[:, t % 2, hs, :], M[:, t % 2, hs, :], cbm[:].unsqueeze(1).broadcast_to([P, 4, P]),
                                      ALU.mult).then_inc(S.M, 1)
                dve.wait_ge(S.xtok, t + 1)
                if t >= 2 and t % 2 == 0:
                    dve.wait_ge(S.dtxe, t // 2)
                dve.tensor_tensor(heads(dtx[:, t % 2, :]), heads(bank[2][:]),
                                  dt_half[:, g % 2, j, :].unsqueeze(2).broadcast_to([P, H, HD]), ALU.mult).then_inc(S.dtx, 1)
                if t >= 2:
                    dve.wait_ge(S.y, t - 1)
                dve.tensor_tensor(heads(xD[:, t % 2, :]), heads(bank[2][:]),
                                  d8[:].unsqueeze(2).broadcast_to([P, H, HD]), ALU.mult).then_inc(S.xD, 1)

            def sum_y(t):
                dve.wait_ge(S.y_mm, t + 1)
                dve.wait_ge(S.xD, t + 1)
                if t:
                    dve.wait_ge(S.yz, t)
                dve.tensor_tensor(y, bank[4][:], xD[:, t % 2, :], ALU.add).then_inc(S.y, 1)
                if t % 2:
                    dve.wait_ge(S.off_mm, t // 2 + 1)
                    dve.tensor_tensor(heads(off), heads(bank[7][:]), edec[:, t % 2, :].unsqueeze(2).broadcast_to([P, H, HD]),
                                      ALU.mult).then_inc(S.off, 1)

            def y_lo(t):
                dve.wait_ge(S.yhi, t + 1)
                dve.tensor_tensor(yTl[:], bank[6][:].rearrange("p (k n) -> p k n", k=KI), as_f32(yTh[:]),
                                  ALU.subtract).then_inc(S.ylo, 1)

            def add_ssd(t):
                dve.wait_ge(S.o, t + 1)
                dve.wait_ge(S.ry, t + 1)
                dve.scalar_tensor_tensor(out=x[:, t, :], in0=bank[7][:, 0:D], scalar=ry[:, t % 2:t % 2 + 1], in1=x[:, t, :],
                                         op0=ALU.mult, op1=ALU.add).then_inc(S.added, 1)

            g_stats(0)
            g_normal(0)
            n_lo(0, 0)
            n_lo(0, 1)
            for j in range(G):
                z_silu(j)
            dt_chain(0, 0)
            dt_chain(0, 1)
            for k in range(NC):
                conv(k)
                if k:
                    conv_silu(k - 1)
            conv_silu(NC - 1)
            for t in range(T + 2):
                g, j = divmod(t, G)
                more = g + 1 < NG
                zs_, cs_ = (Z_AT[j], C_AT[j]) if more else ([], [])
                if t < T:
                    mix(t)
                if j == 0 and more:
                    g_stats(g + 1)
                    g_normal(g + 1)
                if t >= 2:
                    y_lo(t - 2)
                if 1 <= t <= T:
                    sum_y(t - 1)
                for k in cs_:
                    conv(NC * (g + 1) + k)
                for k in cs_:
                    conv_silu(NC * (g + 1) + k)
                if t >= 2:
                    add_ssd(t - 2)
                if j == 0 and more:
                    n_lo(g + 1, 0)
                    n_lo(g + 1, 1)
                for k in zs_:
                    z_silu(G * (g + 1) + k)
                if more and j == 2:
                    dt_chain(g + 1, 0)
                    dt_chain(g + 1, 1)

            def second_ready(t):
                dve.wait_ge(S.added, t + 1)

            ffn(FFN[1], False, second_ready)

        @block.tensor
        def _(pe):
            def product(out_ap, lhs, rhs, first=True, last=True):
                pe.matmul(out_ap, lhs[0], rhs[0], start=first, stop=False)
                pe.matmul(out_ap, lhs[0], rhs[1], start=False, stop=False)
                return pe.matmul(out_ap, lhs[1], rhs[0], start=False, stop=last)

            def x_turn(F, t, s):
                pe.wait_ge(F.xn, t + 1)
                if not isinstance(t, int) or t >= 1:
                    pe.wait_ge(F.xlo, t)
                for k in range(KD):
                    ins = pe.transpose(bank[7][:, k * P:(k + 1) * P], xn[:, s, k * P:(k + 1) * P], ident[:])
                ins.then_inc(F.xT, 1)

            def gate_up(F, q, r, t, s, e, first):
                if not isinstance(q, int) or q >= 3:
                    pe.wait_ge(F.hidden, count(q - 3))
                pe.wait_ge(F.xlo, t + 1)
                if first:
                    pe.wait_ge(raw_lo, e + 2)
                c0, n = (0, CG + E) if e == SH else (CG + E + e * CG, CG)
                for k in range(KD):
                    ins = product(bank[r % 3][:, 0:n], (xTh[:, s, k, :], xTl[:, s, k, :]),
                                  (w1h[:, k, c0:c0 + n], w1l[:, k, c0:c0 + n]), k == 0, k == KD - 1)
                ins.then_inc(F.gate_up, 1)

            def h_turn(F, q, r):
                pe.wait_ge(F.hidden, count(q))
                if not isinstance(q, int) or q >= 2:
                    pe.wait_ge(F.hlo, count(q - 2))
                pe.transpose(bank[3 + r % 2][:, 0:P], hid[:, r % 3, :], ident[:]).then_inc(F.hT, 1)

            def down(F, q, r, s, e, t):
                pe.wait_ge(F.hlo, count(q))
                if e == SH and (not isinstance(t, int) or t >= 2):
                    pe.wait_ge(F.added, t - 1)
                product(bank[5 + s][:, 0:D], (hTh[:, r % 3, :], hTl[:, r % 3, :]),
                        (w2h[:, e + 1, :], w2l[:, e + 1, :]), e == SH, e == E - 1).then_inc(F.down, 1)

            def ffn(F, first):
                x_turn(F, 0, 0)
                gate_up(F, 0, 0, 0, 0, SH, first)
                h_turn(F, 0, 0)

                def tile(t, s, fresh):
                    q0 = t * NSTEP + BEFORE
                    last = isinstance(t, int) and t == T - 1
                    for j, e in enumerate(ORDER):
                        q, r = q0 + j, s * NSTEP + BEFORE + j
                        if j == 3 and not last:
                            x_turn(F, t + 1, 1 - s)
                        if not (last and e == SH):
                            of = (t + 1, 1 - s) if e == SH else (t, s)
                            gate_up(F, q, r, *of, e, fresh)
                        if not isinstance(q, int) or real(q - 2):
                            h_turn(F, q - 2, r - 2)
                        if not isinstance(q, int) or real(q - 3):
                            down_of(F, q - 3, r - 3, t, s, j - 3)

                def down_of(F, q, r, t, s, j):
                    if j < 0:
                        e = ORDER[NSTEP + j]
                        down(F, q, r, s if e == SH else 1 - s, e, t)
                    else:
                        e = ORDER[j]
                        down(F, q, r, 1 - s if e == SH else s, e, t + 1)

                for s in range(2):
                    tile(s, s, first and s == 0)
                with pe.Fori(1, T // 2 - 1) as i:
                    for s in range(2):
                        tile(2 * i + s, s, False)
                for s in range(2):
                    tile(T - 2 + s, s, False)
                for n in range(3):
                    q = LAST + 1 + n
                    r = q - NSTEP * (T - 2)
                    if real(q - 2):
                        h_turn(F, q - 2, r - 2)
                    down_of(F, q - 3, r - 3, T - 1, 1, NSTEP - 3 + n) if real(q - 3) else None

            pe.wait_ge(const_done, 10)
            ffn(FFN[0], True)

            pe.wait_ge(FFN[0].added, T)
            pe.wait_ge(const_done, 13)
            pe.wait_ge(raw_lo, len(chunks))
            last_read = {}

            def reuse(b, sem_, value):
                if b in last_read:
                    pe.wait_ge(*last_read[b])
                last_read[b] = (sem_, value)

            def n_turn(g):
                for pair in range(2):
                    b = 7 - 2 * pair
                    reuse(b, S.nlo, 2 * g + pair + 1)
                    pe.wait_ge(S.xn, G * g + 2 * pair + 2)
                    for k in range(KD):
                        for v in range(2):
                            c = k * 2 * P + v * P
                            ins = pe.transpose(bank[b][:, c:c + P], gxn[:, 2 * pair + v, k * P:(k + 1) * P], ident[:])
                    ins.then_inc(S.nT, 1)

            def conv_mm(i):
                g, k_ = divmod(i, NC)
                c0 = DI + H + CONV_ORDER[k_] * P
                pe.wait_ge(S.nlo, 2 * g + 2)
                reuse(5, conv_free, i + 1)
                for k in range(KD):
                    ins = product(bank[5][:], (wih[:, k, c0:c0 + P], wil[:, k, c0:c0 + P]),
                                  (nTh[:, k, :], nTl[:, k, :]), k == 0, k == KD - 1)
                ins.then_inc(S.conv, 1)

            def z_mm(i):
                g, j = divmod(i, G)
                pe.wait_ge(S.nlo, 2 * g + 2)
                cols = slice(j * P, (j + 1) * P)
                for half in range(2):
                    reuse(5 + half, S.zs, 2 * i + half + 1)
                    for k in range(KD):
                        lhs = (nTh[:, k, cols], nTl[:, k, cols])
                        w = slice(0, ZC) if half == 0 else slice(ZC, ZC + D)
                        ins = product(bank[5 + half][:, 0:ZC if half == 0 else D], lhs, (wih[:, k, w], wil[:, k, w]),
                                      k == 0, k == KD - 1)
                    ins.then_inc(S.z, 1)

            def chunk_in(t):
                g, j = divmod(t, G)
                cols = slice(j * P, (j + 1) * P)
                pe.wait_ge(S.decay, 2 * (t + 1))
                if t:
                    pe.wait_ge(S.exp, 2 * t)
                for half in range(2):
                    hs = slice(4 * half, 4 * half + 4)
                    pe.matmul(bank[half][:], below_r[:], rh[:, hs, :].rearrange("p h n -> p (h n)"), start=True, stop=False)
                    ins = pe.matmul(bank[half][:], below_r[:], rl[:, hs, :].rearrange("p h n -> p (h n)"), start=False, stop=True)
                ins.then_inc(S.seg, 1)
                if j == 0:
                    pe.wait_ge(S.xc, NC * (g + 1))
                if t:
                    pe.wait_ge(S.cbm, t)
                    pe.wait_ge(S.btok, (t + 1) // 2)
                pe.matmul(bank[3][:, P:P + H], below[:] if t % 2 == 0 else upto[:], dA[:, g % 2, j, :], start=True, stop=True)
                if t % 2 == 0:
                    pe.transpose(bank[3][:, 256:256 + N], BT[:, g % 2, cols], ident[0:N, 0:N])
                pe.matmul(bank[3][:, 0:P], BT[:, g % 2, cols], CT[:, g % 2, cols], start=True, stop=True).then_inc(S.misc, 1)
                if t:
                    pe.wait_ge(S.xD, t)
                for c in range(KI):
                    ins = pe.transpose(bank[2][:, c * P:(c + 1) * P], xc[:, g % 2, c, cols], ident[:])
                ins.then_inc(S.xtok, 1)

            def y_turn(t):
                pe.wait_ge(S.yz, t + 1)
                reuse(6, S.ylo, t + 1)
                for c in range(KI):
                    ins = pe.transpose(bank[6][:, c * P:(c + 1) * P], yz[:, t % 2, c * P:(c + 1) * P], ident[:])
                ins.then_inc(S.yT, 1)

            def y_sum(t):
                g, j = divmod(t, G)
                pe.wait_ge(S.M, 2 * (t + 1))
                pe.wait_ge(S.dtx, t + 1)
                if t:
                    pe.wait_ge(S.y, t)
                for h in range(H):
                    ins = pe.matmul(bank[4][:, h * HD:(h + 1) * HD], M[:, t % 2, h, :], dtx[:, t % 2, h * HD:(h + 1) * HD],
                                    start=True, stop=True)
                ins.then_inc(S.y_mm, 1)
                if t % 2 == 0:
                    pe.wait_ge(S.dtxe, t // 2 + 1)
                    pe.wait_ge(S.btok, t // 2 + 1)
                    reuse(7, S.state, t // 2 + 1)
                    pe.matmul(bank[7][0:N, :], Btok[:], dtxe, start=True, stop=True).then_inc(S.carry, 1)
                else:
                    pe.wait_ge(S.state, t // 2 + 1)
                    reuse(7, S.off, t // 2 + 1)
                    pe.matmul(bank[7][:], CT[:, g % 2, j * P:(j + 1) * P], state[:], start=True, stop=True).then_inc(S.off_mm, 1)

            def o_mm(t):
                pe.wait_ge(S.ylo, t + 1)
                reuse(7, S.added, t + 1)
                for c in range(KI):
                    ins = product(bank[7][:, 0:D], (yTh[:, c, :], yTl[:, c, :]), (woh[:, c, :], wol[:, c, :]), c == 0, c == KI - 1)
                ins.then_inc(S.o, 1)

            n_turn(0)
            for j in range(G):
                z_mm(j)
            for k in range(NC):
                conv_mm(k)
            for t in range(T + 2):
                g, j = divmod(t, G)
                more = g + 1 < NG
                zs_, cs_ = (Z_AT[j], C_AT[j]) if more else ([], [])
                if t < T:
                    chunk_in(t)
                if t >= 2:
                    y_turn(t - 2)
                for k in cs_[:1]:
                    conv_mm(NC * (g + 1) + k)
                if 1 <= t <= T:
                    y_sum(t - 1)
                for k in cs_[1:]:
                    conv_mm(NC * (g + 1) + k)
                if t >= 2:
                    o_mm(t - 2)
                if j == 0 and more:
                    n_turn(g + 1)
                for k in zs_:
                    z_mm(G * (g + 1) + k)
            pe.wait_ge(S.added, T)
            ffn(FFN[1], False)


def kernel(L0_attn_u, L0_attn_W_in, L0_attn_conv_w, L0_attn_conv_b, L0_attn_dt_bias, L0_attn_A_log,
           L0_attn_D_param, L0_attn_norm_w, L0_attn_W_out, L0_ffn_router_w, L0_ffn_gate_up_w, L0_ffn_down_w,
           L0_ffn_shared_gate_w, L0_ffn_shared_up_w, L0_ffn_shared_down_w):
    import numpy as np
    import concourse.bacc as bacc
    from concourse.bass_utils import run_bass_kernel_spmd

    u = np.asarray(L0_attn_u)
    w_in = np.asarray(L0_attn_W_in)
    half = DI // 2
    arrays = {
        "u": u.reshape(-1, D),
        "wg_up": L0_ffn_gate_up_w,
        "w_down": L0_ffn_down_w,
        "w_sh_gate": L0_ffn_shared_gate_w,
        "w_sh_up": L0_ffn_shared_up_w,
        "w_sh_down": L0_ffn_shared_down_w,
        "w_router": L0_ffn_router_w,
        "w_in_t": np.concatenate([w_in[:half], w_in[-H:], w_in[half:-H]], axis=0).T,
        "w_out_t": np.asarray(L0_attn_W_out).T,
        "conv_w": np.asarray(L0_attn_conv_w).reshape(NC, P, TAPS).transpose(1, 0, 2),
        "conv_b": np.asarray(L0_attn_conv_b).reshape(NC, P).T,
        "dt_bias": L0_attn_dt_bias,
        "a_log": L0_attn_A_log,
        "d_param": L0_attn_D_param,
        "norm_w": np.asarray(L0_attn_norm_w).reshape(KI, P).T,
    }
    nc = bacc.Bacc("TRN2", target_bir_lowering=False, num_devices=1)
    feeds, args = {}, []
    for name, a in arrays.items():
        a = np.ascontiguousarray(a)
        feeds[f"{name}_dram"] = a
        args.append(nc.dram_tensor(f"{name}_dram", a.shape, mybir.dt.from_np(a.dtype), kind="ExternalInput").ap())
    args.append(nc.dram_tensor("out_dram", (u.size // D, D), F32, kind="ExternalOutput").ap())
    macaron_kernel(nc, *args)
    r = run_bass_kernel_spmd(nc, [feeds], core_ids=[0])
    return r.results[0]["out_dram"].reshape(u.shape)
```

```python
from collections import namedtuple
from contextlib import ExitStack

import concourse.bass as bass
from concourse import mybir

F32 = mybir.dt.float32
F32R = mybir.dt.float32r
U32 = mybir.dt.uint32
ACT = mybir.ActivationFunctionType
ALU = mybir.AluOpType

P = 128
D = 256
KD = D // P
E = 8
I = 128
CG = 2 * I
H = 8
HD = 64
N = 64
DI = H * HD
KI = DI // P
TAPS = 4
SEQ = 256
G = 4
GT = G * P
NC = 5
EPS = 1e-5
ZC = D + H
CONV_ORDER = [4, 0, 1, 2, 3]
DT_OPS = 17
Z_AT = [[0], [1, 2], [3], []]
C_AT = [[], [0], [1, 2], [3, 4]]
ATANH = [1.0 / k for k in (15, 13, 11, 9, 7, 5, 3)]

SH = -1
ORDER = [0, 1, 2, 3, 4, SH, 5, 6, 7]
NSTEP = len(ORDER)
AT_SH = ORDER.index(SH)
BEFORE = NSTEP - AT_SH
TURN, DOWN = 2, 4


def macaron_kernel(nc, u, wg_up, w_down, w_sh_gate, w_sh_up, w_sh_down, w_router, w_in_t, w_out_t,
                   conv_w, conv_b, dt_bias, a_log, d_param, norm_w, out):
    T = u.shape[0] // P
    NG = T // G
    LAST = BEFORE + NSTEP * T - 1
    EMPTY = [*range(1, BEFORE), BEFORE + NSTEP * (T - 1) + AT_SH]

    def real(q):
        return 0 <= q <= LAST and q not in EMPTY

    def count(q):
        if isinstance(q, int):
            return sum(real(k) for k in range(q + 1))
        return q + 2 - BEFORE

    u_v = u.rearrange("(t p) d -> p t d", p=P)
    out_v = out.rearrange("(t p) d -> p t d", p=P)

    with ExitStack() as ctx:
        def sb(name, shape, dt=F32):
            return ctx.enter_context(nc.sbuf_tensor(name, shape, dt))

        def sem(name):
            return ctx.enter_context(nc.semaphore(name))

        bank = [ctx.enter_context(nc.psum_tensor(f"bank{i}", [P, 512], F32)) for i in range(8)]

        x = sb("x", [P, T, D])
        w1h, w1l = sb("w1h", [P, KD, CG + E + E * CG], F32R), sb("w1l", [P, KD, CG + E + E * CG], F32R)
        w2h, w2l = sb("w2h", [P, 1 + E, D], F32R), sb("w2l", [P, 1 + E, D], F32R)
        NIN = w_in_t.shape[1]
        wih, wil = sb("wih", [P, KD, NIN], F32R), sb("wil", [P, KD, NIN], F32R)
        woh, wol = sb("woh", [P, KI, D], F32R), sb("wol", [P, KI, D], F32R)
        ident = sb("ident", [P, P])
        below = sb("below", [P, P])
        below_r = sb("below_r", [P, P], F32R)
        upto = sb("upto", [P, P])
        quarter = sb("quarter", [P, P])
        iota8 = sb("iota8", [P, E])
        half_neg = sb("half_neg", [P, G])
        cw, cb = sb("cw", [P, NC, TAPS]), sb("cb", [P, NC])
        nw = sb("nw", [P, KI])
        bias8, alog8, a8, d8 = sb("bias8", [P, H]), sb("alog8", [P, H]), sb("a8", [P, H]), sb("d8", [P, H])

        st6, mv = sb("st6", [P, 2, 6]), sb("mv", [P, 2, 2])
        ve, rstd = sb("ve", [P, 2]), sb("rstd", [P, 2])
        scratch = sb("scratch", [P, 4 * DI])
        turned_hi, turned_lo = sb("turned_hi", [P, KD * GT], F32R), sb("turned_lo", [P, KD * GT], F32R)
        xn = scratch[:, 0:2 * D].rearrange("p (s d) -> p s d", s=2)
        sil = scratch[:, 2 * D:2 * D + 3 * I].rearrange("p (s d) -> p s d", s=3)
        hid = scratch[:, 2 * D + 3 * I:2 * D + 6 * I].rearrange("p (s d) -> p s d", s=3)
        xTh, xTl = (a[:, 0:2 * D].rearrange("p (s k n) -> p s k n", s=2, k=KD) for a in (turned_hi, turned_lo))
        hTh, hTl = (a[:, 2 * D:2 * D + 3 * P].rearrange("p (s n) -> p s n", s=3) for a in (turned_hi, turned_lo))
        lg, top, topi, topf = sb("lg", [P, 2, E]), sb("top", [P, E]), sb("topi", [P, E], U32), sb("topf", [P, 2])
        one1, one2, th8, p2 = sb("one1", [P, E]), sb("one2", [P, E]), sb("th8", [P, E]), sb("p2", [P, E])
        prob = sb("prob", [P, 2, E])

        gst, gmv = sb("gst", [P, G, 6]), sb("gmv", [P, G, 2])
        gve, grstd = sb("gve", [P, G]), sb("grstd", [P, G])
        gxn = sb("gxn", [P, G, D])
        nTh, nTl = (a[:].rearrange("p (k n) -> p k n", k=KD) for a in (turned_hi, turned_lo))
        cin, cacc = sb("cin", [P, 2, GT]), sb("cacc", [P, 2, GT])
        cth = cin
        xc = sb("xc", [P, 2, KI, GT])
        BT, CT = sb("BT", [N, 2, GT]), sb("CT", [N, 2, GT])
        zs = sb("zs", [P, 2, G, DI])
        COLS = CG + E
        SLOT = KD * COLS + D
        half = 2 * KI * GT // SLOT
        room = [xc[:].rearrange("p a b c -> p (a b c)"), zs[:].rearrange("p a b c -> p (a b c)")]
        slots = [room[i // half][:, (i % half) * SLOT:(i % half + 1) * SLOT] for i in range(2 * half)]
        NSLOT = len(slots)
        raw1 = [a[:, 0:KD * COLS].rearrange("p (k n) -> p k n", k=KD) for a in slots]
        raw2 = [a[:, KD * COLS:SLOT] for a in slots]
        dtr = sb("dtr", [P, 2, G, H])
        dtv, dtu, dtn = sb("dtv", [P, G, H]), sb("dtu", [P, G, H]), sb("dtn", [P, G, H])
        dtd, dts, dts2, dtq = sb("dtd", [P, G, H]), sb("dts", [P, G, H]), sb("dts2", [P, G, H]), sb("dtq", [P, G, H])
        dt_half = sb("dt_half", [P, 2, G, H])
        dA = sb("dA", [P, 2, G, H])
        dAh, dAl = sb("dAh", [P, 2, G, H], F32R), sb("dAl", [P, 2, G, H], F32R)
        rh, rl = sb("rh", [P, H, P], F32R), sb("rl", [P, H, P], F32R)
        M = sb("M", [P, 2, H, P])
        edec = sb("edec", [P, 2, H])
        cbm = sb("cbm", [P, P])
        dtx = sb("dtx", [P, 2, DI])
        y, off, sq, dtxe = (scratch[:, i * DI:(i + 1) * DI] for i in range(4))
        xD = sb("xD", [P, 2, DI])
        Btok, state = sb("Btok", [P, N]), sb("state", [N, DI])
        yz, ss = sb("yz", [P, 2, DI]), sb("ss", [P, 2])
        vy, ry = sb("vy", [P, 2]), sb("ry", [P, 2])
        yTh, yTl = sb("yTh", [P, KI, P], F32R), sb("yTl", [P, KI, P], F32R)

        x_first = sem("x_first")
        x_in = [sem(f"x_in{i}") for i in range(NG)]
        par_in = sem("par_in")
        raw_in = [sem(f"raw_in{i}") for i in range(NSLOT)]
        w1_hi, w1_lo = sem("w1_hi"), sem("w1_lo")
        w2_split = sem("w2_split")
        late_split = sem("late_split")
        const_done = sem("const_done")
        a8_done = sem("a8_done")
        stored = sem("stored")

        def family(prefix, names):
            names = names.split()
            return namedtuple("Signals", names)(*[sem(f"{prefix}_{n}") for n in names])

        FFN = [family(f"f{f}", "stats var rstd xn xT xhi xlo gate_up silu hidden hT hhi hlo down logits route tanh "
                      "prob added") for f in range(2)]
        S = family("s", "stats var rstd xn nT nhi nlo conv cin tap conv_tanh xc z z_tanh zs dt dt_raw dt_exp dA decay seg "
                   "misc xtok exp edec cbm M dtx xD btok dtxe y_mm carry state off off_mm y yoff yz sumsq vy ry yT yhi "
                   "ylo o added")
        conv_free = sem("conv_free")
        share_step = sem("share_step")
        scaled = sem("scaled")

        chunks = []
        for e in range(1 + E):
            c0 = 0 if e == 0 else CG + E + (e - 1) * CG
            n = CG + E if e == 0 else CG
            chunks.append(("expert", e, c0, n))
        for c0 in range(0, NIN, COLS):
            chunks.append(("in", None, c0, min(COLS, NIN - c0)))
        for k in range(0, KI, KD):
            chunks.append(("out", None, k, D))
        LATE = 1 + E

        def load_chunk(sp, c):
            kind, e, c0, n = chunks[c]
            r = c % NSLOT
            old = c - NSLOT
            if 0 <= old < LATE:
                sp.wait_ge(w1_lo, old + 1)
                sp.wait_ge(w2_split, 2 * (old + 1))
            elif old >= LATE:
                sp.wait_ge(late_split, 2 * (old - LATE + 1))
            if kind == "expert":
                if e == 0:
                    for k in range(KD):
                        rows = slice(k * P, (k + 1) * P)
                        sp.dma_start(raw1[r][:, k, 0:I], w_sh_gate[rows, :]).then_inc(raw_in[r], 16)
                        sp.dma_start(raw1[r][:, k, I:CG], w_sh_up[rows, :]).then_inc(raw_in[r], 16)
                        sp.dma_start(raw1[r][:, k, CG:CG + E], w_router[rows, :]).then_inc(raw_in[r], 16)
                    sp.dma_start(raw2[r], w_sh_down).then_inc(raw_in[r], 16)
                else:
                    sp.dma_start(raw1[r][:, :, 0:CG], wg_up[e - 1].rearrange("(k p) f -> p k f", p=P)).then_inc(raw_in[r], 16)
                    sp.dma_start(raw2[r], w_down[e - 1]).then_inc(raw_in[r], 16)
            elif kind == "in":
                sp.dma_start(raw1[r][:, :, 0:n], w_in_t.rearrange("(k p) f -> p k f", p=P)[:, :, c0:c0 + n]).then_inc(raw_in[r], 16)
            else:
                sp.dma_start(raw1[r][:, :, 0:D], w_out_t.rearrange("(k p) f -> p k f", p=P)[:, c0:c0 + KD, :]).then_inc(raw_in[r], 16)

        def landed(eng, c):
            loads = [1 if chunks[k][0] != "expert" else 3 * KD + 1 if k == 0 else 2 for k in range(c % NSLOT, c + 1, NSLOT)]
            eng.wait_ge(raw_in[c % NSLOT], 16 * sum(loads))

        def as_f32(ap):
            return ap.bitcast(F32)

        block = ctx.enter_context(nc.Block())

        @block.sync
        def _(sp):
            sp.dma_start(x[:, 0:1, :], u_v[:, 0:1, :]).then_inc(x_first, 16)
            load_chunk(sp, 0)
            load_chunk(sp, 1)
            sp.dma_start(x[:, 1:G, :], u_v[:, 1:G, :]).then_inc(x_in[0], 16)
            for c in range(2, 1 + E):
                load_chunk(sp, c)
            for i in range(1, NG):
                sp.dma_start(x[:, G * i:G * i + G, :], u_v[:, G * i:G * i + G, :]).then_inc(x_in[i], 16)
            for c in range(LATE, len(chunks)):
                load_chunk(sp, c)
            with sp.Fori(0, T) as t:
                sp.wait_ge(FFN[1].added, t + 1)
                sp.dma_start(out_v[:, bass.ds(t, 1), :], x[:, bass.ds(t, 1), :]).then_inc(stored, 16)
            sp.wait_ge(stored, 16 * T)

        @block.gpsimd
        def _(pool):
            pool.memset(ident[:], 0.0).then_inc(const_done, 1)
            pool.memset(upto[:], 0.0).then_inc(const_done, 1)
            pool.memset(quarter[:], 0.0).then_inc(const_done, 1)
            pool.memset(below[:], 0.0).then_inc(const_done, 1)
            pool.memset(half_neg[:], -0.5).then_inc(const_done, 1)
            pool.wait_ge(const_done, 5)
            pool.affine_select(out=ident[:], in_=ident[:], compare_op=ALU.not_equal, fill=1.0, base=0,
                               pattern=[[-1, P]], channel_multiplier=1).then_inc(const_done, 1)
            pool.affine_select(out=upto[:], in_=upto[:], compare_op=ALU.is_gt, fill=1.0, base=0,
                               pattern=[[-1, P]], channel_multiplier=1).then_inc(const_done, 1)
            pool.affine_select(out=quarter[:], in_=quarter[:], compare_op=ALU.is_gt, fill=0.25, base=0,
                               pattern=[[-1, P]], channel_multiplier=1).then_inc(const_done, 1)
            pool.affine_select(out=below[:], in_=below[:], compare_op=ALU.is_ge, fill=1.0, base=0,
                               pattern=[[1, P]], channel_multiplier=-1).then_inc(const_done, 1)
            pool.iota(iota8[:], pattern=[[1, E]], base=0, channel_multiplier=0,
                      allow_small_or_imprecise_dtypes=True).then_inc(const_done, 1)

            def root(F, t, s):
                pool.wait_ge(F.var, t + 1)
                pool.tensor_tensor(rstd[:, s:s + 1], ve[:, s:s + 1], half_neg[:, 0:1], ALU.pow).then_inc(F.rstd, 1)

            def copy(to, of):
                return pool.tensor_scalar(to, of, 1.0, 0.0, ALU.mult, ALU.add)

            def split_w2(e):
                raw = raw2[e % NSLOT]
                landed(pool, e)
                copy(w2h[:, e, :], raw).then_inc(w2_split, 1)
                pool.wait_ge(w2_split, 2 * e + 1)
                pool.tensor_tensor(w2l[:, e, :], raw, as_f32(w2h[:, e, :]), ALU.subtract).then_inc(w2_split, 1)

            def split_late(c):
                kind, _, c0, n = chunks[c]
                raw = raw1[c % NSLOT][:, :, 0:n]
                landed(pool, c)
                if kind == "in":
                    hi, lo = wih[:, :, c0:c0 + n], wil[:, :, c0:c0 + n]
                else:
                    hi, lo = woh[:, c0:c0 + KD, :], wol[:, c0:c0 + KD, :]
                    pool.wait_ge(par_in, 96)
                    for k in range(KD):
                        ins = pool.tensor_scalar(raw[:, k, :], raw[:, k, :], nw[:, c0 + k:c0 + k + 1], 0.5, ALU.mult,
                                                 ALU.mult)
                    ins.then_inc(scaled, 1)
                    pool.wait_ge(scaled, c0 // KD + 1)
                copy(hi, raw).then_inc(late_split, 1)
                pool.wait_ge(late_split, 2 * (c - LATE) + 1)
                pool.tensor_tensor(lo, raw, as_f32(hi), ALU.subtract).then_inc(late_split, 1)

            split_w2(0)
            root(FFN[0], 0, 0)
            root(FFN[0], 1, 1)
            for e in range(1, 1 + E):
                split_w2(e)
            for t in range(2, T):
                root(FFN[0], t, t % 2)
                if LATE + t - 2 < len(chunks):
                    split_late(LATE + t - 2)

            def group_root(g):
                pool.wait_ge(S.stats, 2 * G * (g + 1))
                pool.tensor_scalar(gve[:], gmv[:, :, 1], EPS, None, ALU.add).then_inc(S.var, 1)
                pool.wait_ge(S.var, g + 1)
                pool.tensor_tensor(grstd[:], gve[:], half_neg[:], ALU.pow).then_inc(S.rstd, 1)

            def decay(t):
                g, j = divmod(t, G)
                pool.wait_ge(S.dA, 2 * (g + 1))
                if t:
                    pool.wait_ge(S.seg, t)
                for r, a in ((rh, dAh), (rl, dAl)):
                    pool.tensor_tensor(r[:], upto[:].unsqueeze(1).broadcast_to([P, H, P]),
                                       as_f32(a[:, g % 2, j, :]).unsqueeze(2).broadcast_to([P, H, P]),
                                       ALU.mult).then_inc(S.decay, 1)

            def gate(t):
                g, j = divmod(t, G)
                pool.wait_ge(S.y, t + 1)
                if t % 2:
                    pool.wait_ge(S.off, t // 2 + 1)
                    pool.tensor_tensor(y, y, off, ALU.add).then_inc(S.yoff, 1)
                    pool.wait_ge(S.yoff, t // 2 + 1)
                if t >= 2:
                    pool.wait_ge(S.yT, t - 1)
                    pool.wait_ge(S.sumsq, t - 1)
                pool.tensor_tensor(yz[:, t % 2, :], y, zs[:, g % 2, j, :], ALU.mult).then_inc(S.yz, 1)

            def norm_root(t):
                pool.wait_ge(S.sumsq, t + 1)
                pool.tensor_scalar(vy[:, t % 2:t % 2 + 1], ss[:, t % 2:t % 2 + 1], 1.0 / (4 * DI), EPS,
                                   ALU.mult, ALU.add).then_inc(S.vy, 1)
                pool.wait_ge(S.vy, t + 1)
                if t >= 2:
                    pool.wait_ge(S.added, t - 1)
                pool.tensor_tensor(ry[:, t % 2:t % 2 + 1], vy[:, t % 2:t % 2 + 1], half_neg[:, 0:1],
                                   ALU.pow).then_inc(S.ry, 1)

            def scaled_inputs(t):
                pool.wait_ge(S.dtx, t + 1)
                pool.wait_ge(S.edec, t + 1)
                if t >= 2:
                    pool.wait_ge(S.carry, t // 2)
                pool.tensor_tensor(dtxe.rearrange("p (h d) -> p h d", h=H),
                                   dtx[:, t % 2, :].rearrange("p (h d) -> p h d", h=H),
                                   edec[:, t % 2, :].unsqueeze(2).broadcast_to([P, H, HD]),
                                   ALU.mult).then_inc(S.dtxe, 1)

            group_root(0)
            decay(0)
            for t in range(T + 2):
                if t < T and t % 2 == 0:
                    scaled_inputs(t)
                if t < T and t % G == 0 and t // G + 1 < NG:
                    group_root(t // G + 1)
                if 1 <= t <= T:
                    gate(t - 1)
                if t + 1 < T:
                    decay(t + 1)
                if 1 <= t <= T:
                    norm_root(t - 1)

            with pool.Fori(0, T // 2) as i:
                for s in range(2):
                    root(FFN[1], 2 * i + s, s)

        @block.scalar
        def _(act):
            params = [(cw[:], conv_w), (cb[:], conv_b), (nw[:], norm_w),
                      (bias8[:], dt_bias.partition_broadcast(P)), (alog8[:], a_log.partition_broadcast(P)),
                      (d8[:], d_param.partition_broadcast(P))]
            for to, of in params:
                act.dma_start(to, of).then_inc(par_in, 16)

            def split_hi(e):
                landed(act, e)
                _, _, c0, n = chunks[e]
                act.activation(w1h[:, :, c0:c0 + n], raw1[e % NSLOT][:, :, 0:n], ACT.Copy).then_inc(w1_hi, 1)

            def x_hi(F, t, s):
                act.wait_ge(F.xT, t + 1)
                act.activation(xTh[:, s], bank[7][:, 0:D].rearrange("p (k n) -> p k n", k=KD),
                               ACT.Copy).then_inc(F.xhi, 1)

            def silu(F, q, r, t, s, e):
                act.wait_ge(F.gate_up, count(q))
                if not isinstance(q, int) or q >= 3:
                    act.wait_ge(F.hidden, count(q - 3))
                if e == SH:
                    act.activation(sil[:, r % 3, :], bank[r % 3][:, 0:I], ACT.Silu).then_inc(F.silu, 1)
                else:
                    act.wait_ge(F.prob, t + 1)
                    act.activation(sil[:, r % 3, :], bank[r % 3][:, 0:I], ACT.Silu,
                                   scale=prob[:, s, e:e + 1]).then_inc(F.silu, 1)

            def h_hi(F, q, r):
                act.wait_ge(F.hT, count(q))
                if not isinstance(q, int) or q >= 3:
                    act.wait_ge(F.down, count(q - 3))
                act.activation(hTh[:, r % 3, :], bank[3 + r % 2][:, 0:P], ACT.Copy).then_inc(F.hhi, 1)

            def tanh_logits(F, t, s):
                act.wait_ge(F.logits, t + 1)
                act.activation(th8[:], lg[:, s, :], ACT.Tanh, scale=0.5).then_inc(F.tanh, 1)

            def ffn(F, first):
                if first:
                    split_hi(0)
                x_hi(F, 0, 0)
                silu(F, 0, 0, 0, 0, SH)
                tanh_logits(F, 0, 0)
                h_hi(F, 0, 0)

                def tile(t, s, split):
                    q0 = t * NSTEP + BEFORE
                    for j, e in enumerate(ORDER):
                        q, r = q0 + j, s * NSTEP + BEFORE + j
                        last = isinstance(t, int) and t == T - 1
                        if split and e != SH:
                            split_hi(1 + e)
                        if not (last and e == SH):
                            silu(F, q, r, t, s, e)
                        if not isinstance(q, int) or real(q - TURN):
                            h_hi(F, q - TURN, r - TURN)
                        if j == 3 and not last:
                            x_hi(F, t + 1, 1 - s)
                        if e == SH and not last:
                            tanh_logits(F, t + 1, 1 - s)

                for s in range(2):
                    tile(s, s, first and s == 0)
                with act.Fori(1, T // 2 - 1) as i:
                    for s in range(2):
                        tile(2 * i + s, s, False)
                for s in range(2):
                    tile(T - 2 + s, s, False)
                for q in (LAST - 1, LAST):
                    h_hi(F, q, q - NSTEP * (T - 2))

            act.wait_ge(par_in, 16 * len(params))
            act.activation(a8[:], alog8[:], ACT.Exp).then_inc(a8_done, 1)
            ffn(FFN[0], True)

            def n_hi(g, pair):
                act.wait_ge(S.nT, 2 * g + pair + 1)
                if g:
                    act.wait_ge(S.conv, 5 * g)
                    act.wait_ge(S.z, 8 * g)
                src = bank[7 - 2 * pair][:].rearrange("p (k n) -> p k n", k=KD)
                act.activation(nTh[:, :, pair * 2 * P:(pair + 1) * 2 * P], src, ACT.Copy).then_inc(S.nhi, 1)

            def conv_in(i):
                c = CONV_ORDER[i % NC]
                act.wait_ge(S.conv, i + 1)
                if i >= 2:
                    act.wait_ge(S.xc, i - 1)
                act.activation(cin[:, i % 2, :], bank[5][:], ACT.Copy).then_inc(S.cin, 1)
                act.activation(cacc[:, i % 2, :], bank[5][:], ACT.Identity, scale=cw[:, c, TAPS - 1:TAPS],
                               bias=cb[:, c:c + 1]).then_inc(conv_free, 1)

            def conv_tanh(i):
                act.wait_ge(S.tap, (TAPS - 1) * (i + 1))
                act.activation(cth[:, i % 2, :], cacc[:, i % 2, :], ACT.Tanh, scale=0.5).then_inc(S.conv_tanh, 1)

            def z_tanh(i):
                for half in range(2):
                    n = 2 * i + half
                    act.wait_ge(S.z, n + 1)
                    g, j = divmod(i, G)
                    if j == 0 and g >= 2:
                        act.wait_ge(S.yz, G * (g - 1))
                    act.activation(zs[:, g % 2, j, half * D:(half + 1) * D], bank[5 + half][:, 0:D], ACT.Tanh,
                                   scale=0.5).then_inc(S.z_tanh, 1)

            def dt_exp(g):
                act.wait_ge(S.dt, DT_OPS * g + 2)
                act.activation(dtu[:], dtn[:], ACT.Exp).then_inc(S.dt_exp, 1)

            def decays(t):
                act.wait_ge(S.seg, t + 1)
                if t >= 2:
                    act.wait_ge(S.y_mm, t - 1)
                for half in range(2):
                    act.activation(M[:, t % 2, half * 4:half * 4 + 4, :], bank[half][:].rearrange("p (h n) -> p h n", h=4),
                                   ACT.Exp).then_inc(S.exp, 1)
                act.wait_ge(S.misc, t + 1)
                act.activation(edec[:, t % 2, :], bank[3][:, P:P + H], ACT.Exp).then_inc(S.edec, 1)

            def carried(t):
                act.wait_ge(S.carry, t // 2 + 1)
                act.activation(state[:], bank[7][0:N, :], ACT.Copy, scale=0.25).then_inc(S.state, 1)

            def square(t):
                act.wait_ge(S.yz, t + 1)
                if t >= 2:
                    act.wait_ge(S.vy, t - 1)
                if t:
                    act.wait_ge(S.sumsq, t)
                act.activation(sq, yz[:, t % 2, :], ACT.Square, accum_out=ss[:, t % 2:t % 2 + 1]).then_inc(S.sumsq, 1)

            def y_hi(t):
                act.wait_ge(S.yT, t + 1)
                if t:
                    act.wait_ge(S.o, t)
                act.activation(yTh[:], bank[6][:].rearrange("p (k n) -> p k n", k=KI), ACT.Copy).then_inc(S.yhi, 1)

            n_hi(0, 0)
            n_hi(0, 1)
            for j in range(G):
                z_tanh(j)
            dt_exp(0)
            for k in range(NC):
                conv_in(k)
                if k:
                    conv_tanh(k - 1)
            conv_tanh(NC - 1)
            for t in range(T + 2):
                g, j = divmod(t, G)
                more = g + 1 < NG
                zs_, cs_ = (Z_AT[j], C_AT[j]) if more else ([], [])
                if t < T:
                    decays(t)
                if t >= 2:
                    y_hi(t - 2)
                for n, k in enumerate(cs_):
                    conv_in(NC * (g + 1) + k)
                    if n == 0 and t % 2 and t <= T:
                        carried(t - 1)
                if not cs_ and t % 2 and t <= T:
                    carried(t - 1)
                for k in cs_:
                    conv_tanh(NC * (g + 1) + k)
                if j == 0 and more:
                    n_hi(g + 1, 0)
                    n_hi(g + 1, 1)
                for k in zs_:
                    z_tanh(G * (g + 1) + k)
                if more and j == 2:
                    dt_exp(g + 1)
                if 1 <= t <= T:
                    square(t - 1)

            ffn(FFN[1], False)

        @block.vector
        def _(dve):
            def split_lo(e):
                _, _, c0, n = chunks[e]
                dve.wait_ge(w1_hi, e + 1)
                dve.tensor_tensor(w1l[:, :, c0:c0 + n], raw1[e % NSLOT][:, :, 0:n], as_f32(w1h[:, :, c0:c0 + n]),
                                  ALU.subtract).then_inc(w1_lo, 1)

            def stats(F, t, s, ready):
                ready(t)
                dve.bn_stats(st6[:, s, :], x[:, bass.ds(t, 1), :].squeeze(1) if not isinstance(t, int) else x[:, t, :]).then_inc(F.stats, 1)
                dve.drain()
                dve.bn_aggr(mv[:, s, :], st6[:, s, :]).then_inc(F.stats, 1)
                dve.wait_ge(F.stats, 2 * t + 2)
                dve.tensor_scalar(ve[:, s:s + 1], mv[:, s, 1:2], EPS, None, ALU.add).then_inc(F.var, 1)

            def normal(F, t, s):
                dve.wait_ge(F.rstd, t + 1)
                if not isinstance(t, int) or t >= 2:
                    dve.wait_ge(F.xT, t - 1)
                src = x[:, bass.ds(t, 1), :].squeeze(1) if not isinstance(t, int) else x[:, t, :]
                dve.tensor_scalar(xn[:, s, :], src, mv[:, s, 0:1], rstd[:, s:s + 1], ALU.subtract,
                                  ALU.mult).then_inc(F.xn, 1)

            def x_lo(F, t, s):
                dve.wait_ge(F.xhi, t + 1)
                dve.tensor_tensor(xTl[:, s], bank[7][:, 0:D].rearrange("p (k n) -> p k n", k=KD), as_f32(xTh[:, s]),
                                  ALU.subtract).then_inc(F.xlo, 1)

            def hidden(F, q, r, s, e):
                dve.wait_ge(F.silu, count(q))
                if not isinstance(q, int) or q >= 3:
                    dve.wait_ge(F.hT, count(q - 3))
                if e == SH:
                    dve.tensor_copy(lg[:, s, :], bank[r % 3][:, CG:CG + E]).then_inc(F.logits, 1)
                    dve.tensor_tensor(hid[:, r % 3, :], bank[r % 3][:, I:CG], sil[:, r % 3, :],
                                      ALU.mult).then_inc(F.hidden, 1)
                else:
                    dve.scalar_tensor_tensor(out=hid[:, r % 3, :], in0=bank[r % 3][:, I:CG], scalar=prob[:, s, e:e + 1],
                                             in1=sil[:, r % 3, :], op0=ALU.mult, op1=ALU.mult).then_inc(F.hidden, 1)

            def h_lo(F, q, r):
                dve.wait_ge(F.hhi, count(q))
                dve.tensor_tensor(hTl[:, r % 3, :], bank[3 + r % 2][:, 0:P], as_f32(hTh[:, r % 3, :]),
                                  ALU.subtract).then_inc(F.hlo, 1)

            def route(F, t, s):
                n = 5 * t
                dve.drain()
                dve.max(top[:], lg[:, s, :]).then_inc(F.route, 1)
                dve.drain()
                dve.max_index(topi[:], top[:], lg[:, s, :]).then_inc(F.route, 1)
                dve.wait_ge(F.route, n + 2)
                dve.tensor_copy(topf[:], topi[:, 0:2]).then_inc(F.route, 1)
                dve.wait_ge(F.route, n + 3)
                dve.tensor_scalar(one1[:], iota8[:], topf[:, 0:1], None, ALU.is_equal).then_inc(F.route, 1)
                dve.wait_ge(F.route, n + 4)
                dve.scalar_tensor_tensor(out=one2[:], in0=iota8[:], scalar=topf[:, 1:2], in1=one1[:],
                                         op0=ALU.is_equal, op1=ALU.add).then_inc(F.route, 1)

            def shares(F, t, s):
                dve.wait_ge(F.tanh, t + 1)
                dve.wait_ge(F.route, 5 * t + 5)
                dve.scalar_tensor_tensor(out=p2[:], in0=th8[:], scalar=1.0, in1=one2[:], op0=ALU.add,
                                         op1=ALU.mult).then_inc(share_step, 1)
                dve.wait_ge(share_step, t + 1 + (0 if F is FFN[0] else T))
                dve.tensor_scalar(prob[:, s, :], p2[:], 0.5, None, ALU.mult).then_inc(F.prob, 1)

            def add_out(F, t, s):
                q = (t + 1) * NSTEP + BEFORE - 1
                dve.wait_ge(F.down, count(q))
                to = x[:, t, :] if isinstance(t, int) else x[:, bass.ds(t, 1), :].squeeze(1)
                dve.scalar_tensor_tensor(out=to, in0=bank[5 + s][:, 0:D], scalar=0.5, in1=to, op0=ALU.mult,
                                         op1=ALU.add).then_inc(F.added, 1)

            def ffn(F, first, ready):
                stats(F, 0, 0, ready)
                if first:
                    split_lo(0)
                normal(F, 0, 0)
                stats(F, 1, 1, ready)
                x_lo(F, 0, 0)
                hidden(F, 0, 0, 0, SH)
                route(F, 0, 0)
                h_lo(F, 0, 0)
                shares(F, 0, 0)

                def tile(t, s, split):
                    q0 = t * NSTEP + BEFORE
                    last = isinstance(t, int) and t == T - 1
                    for j, e in enumerate(ORDER):
                        q, r = q0 + j, s * NSTEP + BEFORE + j
                        if split and e != SH:
                            split_lo(1 + e)
                        if not (last and e == SH):
                            hidden(F, q, r, s if e != SH else 1 - s, e)
                        if not isinstance(q, int) or real(q - TURN):
                            h_lo(F, q - TURN, r - TURN)
                        if j == 0 and not last:
                            normal(F, t + 1, 1 - s)
                        if j == 3 and not last:
                            x_lo(F, t + 1, 1 - s)
                        if j == 4 and not (isinstance(t, int) and t == 0):
                            add_out(F, t - 1, 1 - s)
                        if e == SH and not last:
                            route(F, t + 1, 1 - s)
                        if j == AT_SH + 1 and not last:
                            shares(F, t + 1, 1 - s)
                        if j == 7 and not (isinstance(t, int) and t >= T - 2):
                            stats(F, t + 2, s, ready)

                for s in range(2):
                    tile(s, s, first and s == 0)
                with dve.Fori(1, T // 2 - 1) as i:
                    for s in range(2):
                        tile(2 * i + s, s, False)
                for s in range(2):
                    tile(T - 2 + s, s, False)
                for q in (LAST - 1, LAST):
                    h_lo(F, q, q - NSTEP * (T - 2))
                add_out(F, T - 1, 1)

            dve.wait_ge(const_done, 10)
            dve.tensor_copy(below_r[:], below[:]).then_inc(const_done, 1)
            dve.wait_ge(a8_done, 1)
            dve.wait_ge(par_in, 96)
            dve.tensor_scalar(a8[:], a8[:], -1.0, None, ALU.mult).then_inc(const_done, 1)
            dve.tensor_scalar(d8[:], d8[:], 0.5, None, ALU.mult).then_inc(const_done, 1)

            def first_ready(t):
                if isinstance(t, int) and t == 0:
                    dve.wait_ge(x_first, 16)
                if isinstance(t, int) and t == 1:
                    dve.wait_ge(x_in[0], 16)
                if isinstance(t, int) and t == 2:
                    for i in range(1, NG):
                        dve.wait_ge(x_in[i], 16)

            ffn(FFN[0], True, first_ready)

            def g_stats(g):
                for j in range(G):
                    dve.wait_ge(FFN[0].added, G * g + j + 1)
                    if g:
                        dve.wait_ge(S.xn, G * g)
                    dve.bn_stats(gst[:, j, :], x[:, G * g + j, :]).then_inc(S.stats, 1)
                for j in range(G):
                    dve.wait_ge(S.stats, 2 * G * g + G)
                    dve.bn_aggr(gmv[:, j, :], gst[:, j, :]).then_inc(S.stats, 1)

            def g_normal(g):
                dve.wait_ge(S.rstd, g + 1)
                if g:
                    dve.wait_ge(S.nT, 2 * g)
                for j in range(G):
                    dve.tensor_scalar(gxn[:, j, :], x[:, G * g + j, :], gmv[:, j, 0:1], grstd[:, j:j + 1],
                                      ALU.subtract, ALU.mult).then_inc(S.xn, 1)

            def n_lo(g, pair):
                dve.wait_ge(S.nhi, 2 * g + pair + 1)
                cols = slice(pair * 2 * P, (pair + 1) * 2 * P)
                dve.tensor_tensor(nTl[:, :, cols], bank[7 - 2 * pair][:].rearrange("p (k n) -> p k n", k=KD),
                                  as_f32(nTh[:, :, cols]), ALU.subtract).then_inc(S.nlo, 1)

            def z_silu(i):
                g, j = divmod(i, G)
                for half in range(2):
                    dve.wait_ge(S.z_tanh, 2 * i + half + 1)
                    if half == 0:
                        dve.tensor_copy(dtr[:, g % 2, j, :], bank[5][:, D:ZC]).then_inc(S.dt_raw, 1)
                    z = zs[:, g % 2, j, half * D:(half + 1) * D]
                    dve.scalar_tensor_tensor(out=z, in0=z, scalar=1.0,
                                             in1=bank[5 + half][:, 0:D], op0=ALU.add, op1=ALU.mult).then_inc(S.zs, 1)

            def dt_chain(g, part):
                n = DT_OPS * g

                def step(k, ins):
                    ins.then_inc(S.dt, 1)
                    dve.wait_ge(S.dt, n + k)

                gp = g % 2
                if part == 0:
                    dve.wait_ge(S.dt_raw, G * (g + 1))
                    if g:
                        dve.wait_ge(S.dt, n)
                    step(1, dve.tensor_tensor(dtv[:], dtr[:, gp], bias8[:].unsqueeze(1).broadcast_to([P, G, H]), ALU.add))
                    step(2, dve.scalar_tensor_tensor(out=dtn[:], in0=dtv[:], scalar=-1.0, in1=dtv[:], op0=ALU.mult, op1=ALU.min))
                    return
                dve.wait_ge(S.dt_exp, g + 1)
                step(3, dve.tensor_scalar(dtd[:], dtu[:], 2.0, None, ALU.add))
                step(4, dve.reciprocal(dtd[:], dtd[:]))
                step(5, dve.tensor_tensor(dts[:], dtu[:], dtd[:], ALU.mult))
                step(6, dve.tensor_tensor(dts2[:], dts[:], dts[:], ALU.mult))
                step(7, dve.tensor_scalar(dtq[:], dts2[:], ATANH[0], None, ALU.mult))
                k = 8
                for c in ATANH[1:]:
                    step(k, dve.scalar_tensor_tensor(out=dtq[:], in0=dtq[:], scalar=c, in1=dts2[:], op0=ALU.add, op1=ALU.mult))
                    k += 1
                step(k, dve.scalar_tensor_tensor(out=dtq[:], in0=dtq[:], scalar=1.0, in1=dts[:], op0=ALU.add, op1=ALU.mult))
                step(k + 1, dve.tensor_scalar(dtv[:], dtv[:], 0.0, 0.5, ALU.max, ALU.mult))
                if g >= 2:
                    dve.wait_ge(S.misc, G * (g - 1))
                step(k + 2, dve.tensor_tensor(dt_half[:, gp], dtq[:], dtv[:], ALU.add))
                assert k + 3 == DT_OPS
                step(k + 3, dve.scalar_tensor_tensor(out=dA[:, gp], in0=dt_half[:, gp], scalar=2.0,
                                                     in1=a8[:].unsqueeze(1).broadcast_to([P, G, H]), op0=ALU.mult, op1=ALU.mult))
                dve.tensor_copy(dAh[:, gp], dA[:, gp]).then_inc(S.dA, 1)
                dve.wait_ge(S.dA, 2 * g + 1)
                dve.tensor_tensor(dAl[:, gp], dA[:, gp], as_f32(dAh[:, gp]), ALU.subtract).then_inc(S.dA, 1)

            def conv(i):
                g, k = divmod(i, NC)
                c = CONV_ORDER[k]
                dve.wait_ge(conv_free, i + 1)
                a = cacc[:, i % 2, :].rearrange("p (b l) -> p b l", l=SEQ)
                r = cin[:, i % 2, :].rearrange("p (b l) -> p b l", l=SEQ)
                for s in range(1, TAPS):
                    n = (TAPS - 1) * i + s
                    if s > 1:
                        dve.wait_ge(S.tap, n - 1)
                    dve.scalar_tensor_tensor(out=a[:, :, s:SEQ], in0=r[:, :, 0:SEQ - s], scalar=cw[:, c, TAPS - 1 - s:TAPS - s],
                                             in1=a[:, :, s:SEQ], op0=ALU.mult, op1=ALU.add).then_inc(S.tap, 1)

            def conv_silu(i):
                g, k = divmod(i, NC)
                c = CONV_ORDER[k]
                dve.wait_ge(S.conv_tanh, i + 1)
                if g >= 2 and k == 0:
                    dve.wait_ge(S.xtok, G * (g - 1))
                    dve.wait_ge(S.carry, G * (g - 1) // 2)
                    dve.wait_ge(S.off_mm, G * (g - 1) // 2)
                if c < KI:
                    dve.scalar_tensor_tensor(out=xc[:, g % 2, c, :], in0=cth[:, i % 2, :], scalar=1.0, in1=cacc[:, i % 2, :],
                                             op0=ALU.add, op1=ALU.mult).then_inc(S.xc, 1)
                    return
                dve.scalar_tensor_tensor(out=BT[:, g % 2, :], in0=cth[0:N, i % 2, :], scalar=1.0, in1=cacc[0:N, i % 2, :],
                                         op0=ALU.add, op1=ALU.mult)
                dve.scalar_tensor_tensor(out=CT[:, g % 2, :], in0=cth[N:P, i % 2, :], scalar=1.0, in1=cacc[N:P, i % 2, :],
                                         op0=ALU.add, op1=ALU.mult).then_inc(S.xc, 1)

            def heads(ap):
                return ap.rearrange("p (h d) -> p h d", h=H)

            def mix(t):
                g, j = divmod(t, G)
                dve.wait_ge(S.edec, t + 1)
                if t:
                    dve.wait_ge(S.M, 2 * t)
                dve.tensor_tensor(cbm[:], bank[3][:, 0:P], quarter[:], ALU.mult).then_inc(S.cbm, 1)
                if t % 2 == 0:
                    if t:
                        dve.wait_ge(S.carry, t // 2)
                    dve.tensor_copy(Btok[:], bank[3][:, 256:256 + N]).then_inc(S.btok, 1)
                dve.wait_ge(S.cbm, t + 1)
                if t >= 2:
                    dve.wait_ge(S.y_mm, t - 1)
                for half in range(2):
                    dve.wait_ge(S.exp, 2 * t + half + 1)
                    hs = slice(4 * half, 4 * half + 4)
                    dve.tensor_tensor(M[:, t % 2, hs, :], M[:, t % 2, hs, :], cbm[:].unsqueeze(1).broadcast_to([P, 4, P]),
                                      ALU.mult).then_inc(S.M, 1)
                dve.wait_ge(S.xtok, t + 1)
                if t >= 2 and t % 2 == 0:
                    dve.wait_ge(S.dtxe, t // 2)
                dve.tensor_tensor(heads(dtx[:, t % 2, :]), heads(bank[2][:]),
                                  dt_half[:, g % 2, j, :].unsqueeze(2).broadcast_to([P, H, HD]), ALU.mult).then_inc(S.dtx, 1)
                if t >= 2:
                    dve.wait_ge(S.y, t - 1)
                dve.tensor_tensor(heads(xD[:, t % 2, :]), heads(bank[2][:]),
                                  d8[:].unsqueeze(2).broadcast_to([P, H, HD]), ALU.mult).then_inc(S.xD, 1)

            def sum_y(t):
                dve.wait_ge(S.y_mm, t + 1)
                dve.wait_ge(S.xD, t + 1)
                if t:
                    dve.wait_ge(S.yz, t)
                dve.tensor_tensor(y, bank[4][:], xD[:, t % 2, :], ALU.add).then_inc(S.y, 1)
                if t % 2:
                    dve.wait_ge(S.off_mm, t // 2 + 1)
                    dve.tensor_tensor(heads(off), heads(bank[7][:]), edec[:, t % 2, :].unsqueeze(2).broadcast_to([P, H, HD]),
                                      ALU.mult).then_inc(S.off, 1)

            def y_lo(t):
                dve.wait_ge(S.yhi, t + 1)
                dve.tensor_tensor(yTl[:], bank[6][:].rearrange("p (k n) -> p k n", k=KI), as_f32(yTh[:]),
                                  ALU.subtract).then_inc(S.ylo, 1)

            def add_ssd(t):
                dve.wait_ge(S.o, t + 1)
                dve.wait_ge(S.ry, t + 1)
                dve.scalar_tensor_tensor(out=x[:, t, :], in0=bank[7][:, 0:D], scalar=ry[:, t % 2:t % 2 + 1], in1=x[:, t, :],
                                         op0=ALU.mult, op1=ALU.add).then_inc(S.added, 1)

            g_stats(0)
            g_normal(0)
            n_lo(0, 0)
            n_lo(0, 1)
            for j in range(G):
                z_silu(j)
            dt_chain(0, 0)
            dt_chain(0, 1)
            for k in range(NC):
                conv(k)
                if k:
                    conv_silu(k - 1)
            conv_silu(NC - 1)
            for t in range(T + 2):
                g, j = divmod(t, G)
                more = g + 1 < NG
                zs_, cs_ = (Z_AT[j], C_AT[j]) if more else ([], [])
                if t < T:
                    mix(t)
                if j == 0 and more:
                    g_stats(g + 1)
                    g_normal(g + 1)
                if t >= 2:
                    y_lo(t - 2)
                if 1 <= t <= T:
                    sum_y(t - 1)
                for k in cs_:
                    conv(NC * (g + 1) + k)
                for k in cs_:
                    conv_silu(NC * (g + 1) + k)
                if t >= 2:
                    add_ssd(t - 2)
                if j == 0 and more:
                    n_lo(g + 1, 0)
                    n_lo(g + 1, 1)
                for k in zs_:
                    z_silu(G * (g + 1) + k)
                if more and j == 2:
                    dt_chain(g + 1, 0)
                    dt_chain(g + 1, 1)

            def second_ready(t):
                dve.wait_ge(S.added, t + 1)

            ffn(FFN[1], False, second_ready)

        @block.tensor
        def _(pe):
            def product(out_ap, lhs, rhs, first=True, last=True):
                pe.matmul(out_ap, lhs[0], rhs[0], start=first, stop=False)
                pe.matmul(out_ap, lhs[0], rhs[1], start=False, stop=False)
                return pe.matmul(out_ap, lhs[1], rhs[0], start=False, stop=last)

            def x_turn(F, t, s):
                pe.wait_ge(F.xn, t + 1)
                if not isinstance(t, int) or t >= 1:
                    pe.wait_ge(F.xlo, t)
                for k in range(KD):
                    ins = pe.transpose(bank[7][:, k * P:(k + 1) * P], xn[:, s, k * P:(k + 1) * P], ident[:])
                ins.then_inc(F.xT, 1)

            def gate_up(F, q, r, t, s, e, first):
                if not isinstance(q, int) or q >= 3:
                    pe.wait_ge(F.hidden, count(q - 3))
                pe.wait_ge(F.xlo, t + 1)
                if first:
                    pe.wait_ge(w1_lo, e + 2)
                c0, n = (0, CG + E) if e == SH else (CG + E + e * CG, CG)
                for k in range(KD):
                    ins = product(bank[r % 3][:, 0:n], (xTh[:, s, k, :], xTl[:, s, k, :]),
                                  (w1h[:, k, c0:c0 + n], w1l[:, k, c0:c0 + n]), k == 0, k == KD - 1)
                ins.then_inc(F.gate_up, 1)

            def h_turn(F, q, r):
                pe.wait_ge(F.hidden, count(q))
                if not isinstance(q, int) or q >= 2:
                    pe.wait_ge(F.hlo, count(q - 2))
                pe.transpose(bank[3 + r % 2][:, 0:P], hid[:, r % 3, :], ident[:]).then_inc(F.hT, 1)

            def down(F, q, r, s, e, t):
                if F is FFN[0] and isinstance(t, int) and t == 0:
                    pe.wait_ge(w2_split, 2 * (e + 2))
                pe.wait_ge(F.hlo, count(q))
                if e == SH and (not isinstance(t, int) or t >= 2):
                    pe.wait_ge(F.added, t - 1)
                product(bank[5 + s][:, 0:D], (hTh[:, r % 3, :], hTl[:, r % 3, :]),
                        (w2h[:, e + 1, :], w2l[:, e + 1, :]), e == SH, e == E - 1).then_inc(F.down, 1)

            def ffn(F, first):
                x_turn(F, 0, 0)
                gate_up(F, 0, 0, 0, 0, SH, first)
                h_turn(F, 0, 0)

                def tile(t, s, fresh):
                    q0 = t * NSTEP + BEFORE
                    last = isinstance(t, int) and t == T - 1
                    for j, e in enumerate(ORDER):
                        q, r = q0 + j, s * NSTEP + BEFORE + j
                        if j == 2 and not last:
                            x_turn(F, t + 1, 1 - s)
                        if not (last and e == SH):
                            of = (t + 1, 1 - s) if e == SH else (t, s)
                            gate_up(F, q, r, *of, e, fresh)
                        if not isinstance(q, int) or real(q - TURN):
                            h_turn(F, q - TURN, r - TURN)
                        if not isinstance(q, int) or real(q - DOWN):
                            down_of(F, q - DOWN, r - DOWN, t, s, j - DOWN)

                def down_of(F, q, r, t, s, j):
                    if j < 0:
                        e = ORDER[NSTEP + j]
                        down(F, q, r, s if e == SH else 1 - s, e, t if e == SH else t - 1)
                    else:
                        e = ORDER[j]
                        down(F, q, r, 1 - s if e == SH else s, e, t + 1 if e == SH else t)

                for s in range(2):
                    tile(s, s, first and s == 0)
                with pe.Fori(1, T // 2 - 1) as i:
                    for s in range(2):
                        tile(2 * i + s, s, False)
                for s in range(2):
                    tile(T - 2 + s, s, False)
                for n in range(DOWN):
                    q = LAST + 1 + n
                    r = q - NSTEP * (T - 2)
                    if n < TURN:
                        h_turn(F, q - TURN, r - TURN)
                    if real(q - DOWN):
                        down_of(F, q - DOWN, r - DOWN, T - 1, 1, NSTEP - DOWN + n)

            pe.wait_ge(const_done, 10)
            ffn(FFN[0], True)

            pe.wait_ge(FFN[0].added, T)
            pe.wait_ge(const_done, 13)
            pe.wait_ge(late_split, 2 * (len(chunks) - LATE))
            last_read = {}

            def reuse(b, sem_, value):
                if b in last_read:
                    pe.wait_ge(*last_read[b])
                last_read[b] = (sem_, value)

            def n_turn(g):
                for pair in range(2):
                    b = 7 - 2 * pair
                    reuse(b, S.nlo, 2 * g + pair + 1)
                    pe.wait_ge(S.xn, G * g + 2 * pair + 2)
                    for k in range(KD):
                        for v in range(2):
                            c = k * 2 * P + v * P
                            ins = pe.transpose(bank[b][:, c:c + P], gxn[:, 2 * pair + v, k * P:(k + 1) * P], ident[:])
                    ins.then_inc(S.nT, 1)

            def conv_mm(i):
                g, k_ = divmod(i, NC)
                c0 = DI + H + CONV_ORDER[k_] * P
                pe.wait_ge(S.nlo, 2 * g + 2)
                reuse(5, conv_free, i + 1)
                for k in range(KD):
                    ins = product(bank[5][:], (wih[:, k, c0:c0 + P], wil[:, k, c0:c0 + P]),
                                  (nTh[:, k, :], nTl[:, k, :]), k == 0, k == KD - 1)
                ins.then_inc(S.conv, 1)

            def z_mm(i):
                g, j = divmod(i, G)
                pe.wait_ge(S.nlo, 2 * g + 2)
                cols = slice(j * P, (j + 1) * P)
                for half in range(2):
                    reuse(5 + half, S.zs, 2 * i + half + 1)
                    for k in range(KD):
                        lhs = (nTh[:, k, cols], nTl[:, k, cols])
                        w = slice(0, ZC) if half == 0 else slice(ZC, ZC + D)
                        ins = product(bank[5 + half][:, 0:ZC if half == 0 else D], lhs, (wih[:, k, w], wil[:, k, w]),
                                      k == 0, k == KD - 1)
                    ins.then_inc(S.z, 1)

            def chunk_in(t):
                g, j = divmod(t, G)
                cols = slice(j * P, (j + 1) * P)
                pe.wait_ge(S.decay, 2 * (t + 1))
                if t:
                    pe.wait_ge(S.exp, 2 * t)
                for half in range(2):
                    hs = slice(4 * half, 4 * half + 4)
                    pe.matmul(bank[half][:], below_r[:], rh[:, hs, :].rearrange("p h n -> p (h n)"), start=True, stop=False)
                    ins = pe.matmul(bank[half][:], below_r[:], rl[:, hs, :].rearrange("p h n -> p (h n)"), start=False, stop=True)
                ins.then_inc(S.seg, 1)
                if j == 0:
                    pe.wait_ge(S.xc, NC * (g + 1))
                if t:
                    pe.wait_ge(S.cbm, t)
                    pe.wait_ge(S.btok, (t + 1) // 2)
                pe.matmul(bank[3][:, P:P + H], below[:] if t % 2 == 0 else upto[:], dA[:, g % 2, j, :], start=True, stop=True)
                if t % 2 == 0:
                    pe.transpose(bank[3][:, 256:256 + N], BT[:, g % 2, cols], ident[0:N, 0:N])
                pe.matmul(bank[3][:, 0:P], BT[:, g % 2, cols], CT[:, g % 2, cols], start=True, stop=True).then_inc(S.misc, 1)
                if t:
                    pe.wait_ge(S.xD, t)
                for c in range(KI):
                    ins = pe.transpose(bank[2][:, c * P:(c + 1) * P], xc[:, g % 2, c, cols], ident[:])
                ins.then_inc(S.xtok, 1)

            def y_turn(t):
                pe.wait_ge(S.yz, t + 1)
                reuse(6, S.ylo, t + 1)
                for c in range(KI):
                    ins = pe.transpose(bank[6][:, c * P:(c + 1) * P], yz[:, t % 2, c * P:(c + 1) * P], ident[:])
                ins.then_inc(S.yT, 1)

            def y_sum(t):
                g, j = divmod(t, G)
                pe.wait_ge(S.M, 2 * (t + 1))
                pe.wait_ge(S.dtx, t + 1)
                if t:
                    pe.wait_ge(S.y, t)
                for h in range(H):
                    ins = pe.matmul(bank[4][:, h * HD:(h + 1) * HD], M[:, t % 2, h, :], dtx[:, t % 2, h * HD:(h + 1) * HD],
                                    start=True, stop=True)
                ins.then_inc(S.y_mm, 1)
                if t % 2 == 0:
                    pe.wait_ge(S.dtxe, t // 2 + 1)
                    pe.wait_ge(S.btok, t // 2 + 1)
                    reuse(7, S.state, t // 2 + 1)
                    pe.matmul(bank[7][0:N, :], Btok[:], dtxe, start=True, stop=True).then_inc(S.carry, 1)
                else:
                    pe.wait_ge(S.state, t // 2 + 1)
                    reuse(7, S.off, t // 2 + 1)
                    pe.matmul(bank[7][:], CT[:, g % 2, j * P:(j + 1) * P], state[:], start=True, stop=True).then_inc(S.off_mm, 1)

            def o_mm(t):
                pe.wait_ge(S.ylo, t + 1)
                reuse(7, S.added, t + 1)
                for c in range(KI):
                    ins = product(bank[7][:, 0:D], (yTh[:, c, :], yTl[:, c, :]), (woh[:, c, :], wol[:, c, :]), c == 0, c == KI - 1)
                ins.then_inc(S.o, 1)

            n_turn(0)
            for j in range(G):
                z_mm(j)
            for k in range(NC):
                conv_mm(k)
            for t in range(T + 2):
                g, j = divmod(t, G)
                more = g + 1 < NG
                zs_, cs_ = (Z_AT[j], C_AT[j]) if more else ([], [])
                if t < T:
                    chunk_in(t)
                if t >= 2:
                    y_turn(t - 2)
                for k in cs_[:1]:
                    conv_mm(NC * (g + 1) + k)
                if 1 <= t <= T:
                    y_sum(t - 1)
                for k in cs_[1:]:
                    conv_mm(NC * (g + 1) + k)
                if t >= 2:
                    o_mm(t - 2)
                if j == 0 and more:
                    n_turn(g + 1)
                for k in zs_:
                    z_mm(G * (g + 1) + k)
            pe.wait_ge(S.added, T)
            ffn(FFN[1], False)


def kernel(L0_attn_u, L0_attn_W_in, L0_attn_conv_w, L0_attn_conv_b, L0_attn_dt_bias, L0_attn_A_log,
           L0_attn_D_param, L0_attn_norm_w, L0_attn_W_out, L0_ffn_router_w, L0_ffn_gate_up_w, L0_ffn_down_w,
           L0_ffn_shared_gate_w, L0_ffn_shared_up_w, L0_ffn_shared_down_w):
    import numpy as np
    import concourse.bacc as bacc
    from concourse.bass_utils import run_bass_kernel_spmd

    u = np.asarray(L0_attn_u)
    w_in = np.asarray(L0_attn_W_in)
    half = DI // 2
    arrays = {
        "u": u.reshape(-1, D),
        "wg_up": L0_ffn_gate_up_w,
        "w_down": L0_ffn_down_w,
        "w_sh_gate": L0_ffn_shared_gate_w,
        "w_sh_up": L0_ffn_shared_up_w,
        "w_sh_down": L0_ffn_shared_down_w,
        "w_router": L0_ffn_router_w,
        "w_in_t": np.concatenate([w_in[:half], w_in[-H:], w_in[half:-H]], axis=0).T,
        "w_out_t": np.asarray(L0_attn_W_out).T,
        "conv_w": np.asarray(L0_attn_conv_w).reshape(NC, P, TAPS).transpose(1, 0, 2),
        "conv_b": np.asarray(L0_attn_conv_b).reshape(NC, P).T,
        "dt_bias": L0_attn_dt_bias,
        "a_log": L0_attn_A_log,
        "d_param": L0_attn_D_param,
        "norm_w": np.asarray(L0_attn_norm_w).reshape(KI, P).T,
    }
    nc = bacc.Bacc("TRN2", target_bir_lowering=False, num_devices=1)
    feeds, args = {}, []
    for name, a in arrays.items():
        a = np.ascontiguousarray(a)
        feeds[f"{name}_dram"] = a
        args.append(nc.dram_tensor(f"{name}_dram", a.shape, mybir.dt.from_np(a.dtype), kind="ExternalInput").ap())
    args.append(nc.dram_tensor("out_dram", (u.size // D, D), F32, kind="ExternalOutput").ap())
    macaron_kernel(nc, *args)
    r = run_bass_kernel_spmd(nc, [feeds], core_ids=[0])
    return r.results[0]["out_dram"].reshape(u.shape)
```

```python
from collections import namedtuple
from contextlib import ExitStack

import concourse.bass as bass
from concourse import mybir

F32 = mybir.dt.float32
F32R = mybir.dt.float32r
U32 = mybir.dt.uint32
ACT = mybir.ActivationFunctionType
ALU = mybir.AluOpType

P = 128
D = 256
KD = D // P
E = 8
I = 128
CG = 2 * I
H = 8
HD = 64
N = 64
DI = H * HD
KI = DI // P
TAPS = 4
SEQ = 256
G = 4
GT = G * P
NC = 5
EPS = 1e-5
ZC = D + H
CONV_ORDER = [4, 0, 1, 2, 3]
DT_OPS = 17
FIRST = ["n0", "n1", "z00", "z01", "z02", "z03", "c0", "c1", "c2", "c3", "c4", "z10", "z11", "z12", "z13"]
LATER = ["n0", "n1", "z00", "z01", "z02", "z03", "c0", "c1", "z10", "c2", "c3", "c4", "z11", "z12", "z13"]
ATANH = [1.0 / k for k in (15, 13, 11, 9, 7, 5, 3)]


def piece_bank(g, piece):
    if g:
        return 5 + (len(LATER) * (g - 1) + LATER.index(piece)) % 2
    n = FIRST.index(piece)
    return 7 if n < 8 or n % 2 else 5


SH = -1
ORDER = [0, 1, 2, 3, 4, SH, 5, 6, 7]
NSTEP = len(ORDER)
AT_SH = ORDER.index(SH)
BEFORE = NSTEP - AT_SH
TURN, DOWN = 2, 4


def macaron_kernel(nc, u, wg_up, w_down, w_sh_gate, w_sh_up, w_sh_down, w_router, w_in_t, w_out_t,
                   conv_w, conv_b, dt_bias, a_log, d_param, norm_w, out):
    T = u.shape[0] // P
    NG = T // G
    LAST = BEFORE + NSTEP * T - 1
    EMPTY = [*range(1, BEFORE), BEFORE + NSTEP * (T - 1) + AT_SH]

    def real(q):
        return 0 <= q <= LAST and q not in EMPTY

    def count(q):
        if isinstance(q, int):
            return sum(real(k) for k in range(q + 1))
        return q + 2 - BEFORE

    u_v = u.rearrange("(t p) d -> p t d", p=P)
    out_v = out.rearrange("(t p) d -> p t d", p=P)

    with ExitStack() as ctx:
        def sb(name, shape, dt=F32):
            return ctx.enter_context(nc.sbuf_tensor(name, shape, dt))

        def sem(name):
            return ctx.enter_context(nc.semaphore(name))

        bank = [ctx.enter_context(nc.psum_tensor(f"bank{i}", [P, 512], F32)) for i in range(8)]

        x = sb("x", [P, T, D])
        w1h, w1l = sb("w1h", [P, KD, CG + E + E * CG], F32R), sb("w1l", [P, KD, CG + E + E * CG], F32R)
        w2h, w2l = sb("w2h", [P, 1 + E, D], F32R), sb("w2l", [P, 1 + E, D], F32R)
        NIN = w_in_t.shape[1]
        wih, wil = sb("wih", [P, KD, NIN], F32R), sb("wil", [P, KD, NIN], F32R)
        woh, wol = sb("woh", [P, KI, D], F32R), sb("wol", [P, KI, D], F32R)
        ident = sb("ident", [P, P])
        below = sb("below", [P, P])
        below_r = sb("below_r", [P, P], F32R)
        upto = sb("upto", [P, P])
        iota8 = sb("iota8", [P, E])
        half_neg = sb("half_neg", [P, G])
        cw, cb = sb("cw", [P, NC, TAPS]), sb("cb", [P, NC])
        nw = sb("nw", [P, KI])
        bias8, alog8, a8, d8 = sb("bias8", [P, H]), sb("alog8", [P, H]), sb("a8", [P, H]), sb("d8", [P, H])

        st6, mv = sb("st6", [P, 2, 6]), sb("mv", [P, 2, 2])
        ve, rstd = sb("ve", [P, 2]), sb("rstd", [P, 2])
        scratch = sb("scratch", [P, 4 * DI])
        xn = scratch[:, 3 * DI:3 * DI + 2 * D].rearrange("p (s d) -> p s d", s=2)
        M = sb("M", [P, 2, H, P])
        sil, hid = M[:, 0, 0:3, :], M[:, 0, 3:6, :]
        turned_hi, turned_lo = sb("turned_hi", [P, 2 * D + 3 * P], F32R), sb("turned_lo", [P, 2 * D + 3 * P], F32R)
        xTh, xTl = (a[:, 0:2 * D].rearrange("p (s k n) -> p s k n", s=2, k=KD) for a in (turned_hi, turned_lo))
        hTh, hTl = (a[:, 2 * D:2 * D + 3 * P].rearrange("p (s n) -> p s n", s=3) for a in (turned_hi, turned_lo))
        lg, top, topi, topf = sb("lg", [P, 2, E]), sb("top", [P, E]), sb("topi", [P, E], U32), sb("topf", [P, 2])
        one1, one2, th8, p2 = sb("one1", [P, E]), sb("one2", [P, E]), sb("th8", [P, E]), sb("p2", [P, E])
        prob = sb("prob", [P, 2, E])

        gst, gmv = sb("gst", [P, G, 6]), sb("gmv", [P, G, 2])
        gve, grstd = sb("gve", [P, G]), sb("grstd", [P, G])
        gxn = sb("gxn", [P, G, D])
        nTh, nTl = sb("nTh", [P, KD, GT], F32R), sb("nTl", [P, KD, GT], F32R)
        bc = sb("bc", [P, GT])
        xc = sb("xc", [P, 2, KI, GT])
        BT, CT = sb("BT", [N, 2, GT]), sb("CT", [N, 2, GT])
        zs = sb("zs", [P, 2, G, DI])
        COLS = CG + E
        SLOT = KD * COLS + D
        half = 2 * KI * GT // SLOT
        room = [xc[:].rearrange("p a b c -> p (a b c)"), zs[:].rearrange("p a b c -> p (a b c)")]
        slots = [room[i // half][:, (i % half) * SLOT:(i % half + 1) * SLOT] for i in range(2 * half)]
        NSLOT = len(slots)
        raw1 = [a[:, 0:KD * COLS].rearrange("p (k n) -> p k n", k=KD) for a in slots]
        raw2 = [a[:, KD * COLS:SLOT] for a in slots]
        dtr = sb("dtr", [P, G, H])
        dtv, dtu, dtn = sb("dtv", [P, G, H]), sb("dtu", [P, G, H]), sb("dtn", [P, G, H])
        dtd, dts, dts2, dtq = sb("dtd", [P, G, H]), sb("dts", [P, G, H]), sb("dts2", [P, G, H]), sb("dtq", [P, G, H])
        dt = sb("dt", [P, 2, G, H])
        dA = sb("dA", [P, 2, G, H])
        dAh, dAl = sb("dAh", [P, 2, G, H], F32R), sb("dAl", [P, 2, G, H], F32R)
        rh, rl = sb("rh", [P, H, P], F32R), sb("rl", [P, H, P], F32R)
        edec = sb("edec", [P, 4, H])
        cbm = sb("cbm", [P, P])
        dtx = sb("dtx", [P, 2, DI])
        y, off, sq, dtxe = (scratch[:, i * DI:(i + 1) * DI] for i in range(4))
        xD = sb("xD", [P, 2, DI])
        Btok, state = sb("Btok", [P, N]), sb("state", [N, DI])
        yz, ss = sb("yz", [P, 2, DI]), sb("ss", [P, 2])
        vy, ry = sb("vy", [P, 2]), sb("ry", [P, 2])
        yTh, yTl = sb("yTh", [P, KI, P], F32R), sb("yTl", [P, KI, P], F32R)

        x_first = sem("x_first")
        x_in = [sem(f"x_in{i}") for i in range(NG)]
        par_in = sem("par_in")
        raw_in = [sem(f"raw_in{i}") for i in range(NSLOT)]
        w1_hi, w1_lo = sem("w1_hi"), sem("w1_lo")
        w2_split = sem("w2_split")
        late_split = sem("late_split")
        const_done = sem("const_done")
        a8_done = sem("a8_done")
        stored = sem("stored")

        def family(prefix, names):
            names = names.split()
            return namedtuple("Signals", names)(*[sem(f"{prefix}_{n}") for n in names])

        FFN = [family(f"f{f}", "stats var rstd xn xT xhi xlo gate_up silu hidden hT hhi hlo down logits route tanh "
                      "prob added") for f in range(2)]
        S = family("s", "stats var rstd xn nT nhi nlo conv acc tap xc z0 z0_out z1 zs z0_silu dt dt_exp dA decay seg "
                   "misc xtok exp edec cbm M dec dtx xD btok dtxe y_mm carry state off off_mm y yoff yz sumsq vy ry yT yhi "
                   "ylo o added")
        share_step = sem("share_step")
        scaled = sem("scaled")

        chunks = []
        for e in range(1 + E):
            c0 = 0 if e == 0 else CG + E + (e - 1) * CG
            n = CG + E if e == 0 else CG
            chunks.append(("expert", e, c0, n))
        for c0 in range(0, NIN, COLS):
            chunks.append(("in", None, c0, min(COLS, NIN - c0)))
        for k in range(0, KI, KD):
            chunks.append(("out", None, k, D))
        LATE = 1 + E

        def load_shared(eng, k):
            rows = slice(k * P, (k + 1) * P)
            eng.dma_start(raw1[0][:, k, 0:I], w_sh_gate[rows, :]).then_inc(raw_in[0], 16)
            eng.dma_start(raw1[0][:, k, I:CG], w_sh_up[rows, :]).then_inc(raw_in[0], 16)
            eng.dma_start(raw1[0][:, k, CG:CG + E], w_router[rows, :]).then_inc(raw_in[0], 16)

        def load_chunk(sp, c):
            kind, e, c0, n = chunks[c]
            r = c % NSLOT
            old = c - NSLOT
            if 0 <= old < LATE:
                sp.wait_ge(w1_lo, old + 1)
                sp.wait_ge(w2_split, 2 * (old + 1))
            elif old >= LATE:
                sp.wait_ge(late_split, 2 * (old - LATE + 1))
            if kind == "expert":
                if e == 0:
                    load_shared(sp, 0)
                    sp.dma_start(raw2[r], w_sh_down).then_inc(raw_in[r], 16)
                else:
                    sp.dma_start(raw1[r][:, :, 0:CG], wg_up[e - 1].rearrange("(k p) f -> p k f", p=P)).then_inc(raw_in[r], 16)
                    sp.dma_start(raw2[r], w_down[e - 1]).then_inc(raw_in[r], 16)
            elif kind == "in":
                sp.dma_start(raw1[r][:, :, 0:n], w_in_t.rearrange("(k p) f -> p k f", p=P)[:, :, c0:c0 + n]).then_inc(raw_in[r], 16)
            else:
                sp.dma_start(raw1[r][:, :, 0:D], w_out_t.rearrange("(k p) f -> p k f", p=P)[:, c0:c0 + KD, :]).then_inc(raw_in[r], 16)

        def landed(eng, c):
            loads = [1 if chunks[k][0] != "expert" else 3 * KD + 1 if k == 0 else 2 for k in range(c % NSLOT, c + 1, NSLOT)]
            eng.wait_ge(raw_in[c % NSLOT], 16 * sum(loads))

        def x_bank(F, t):
            return 5 if F is FFN[1] and isinstance(t, int) and t == 0 else 7

        def turned_bank(t):
            return 0 if t < T - 1 else 6

        def out_bank(t):
            return 7 if t < T - 1 else 6

        def of_tile(stage, t, first=0, last=T - 1):
            if first <= t <= last:
                stage(t)

        def of_group(stage, g, *piece, first=1):
            if first <= g < NG:
                stage(g, *piece)

        def as_f32(ap):
            return ap.bitcast(F32)

        block = ctx.enter_context(nc.Block())

        @block.sync
        def _(sp):
            sp.dma_start(x[:, 0:1, :], u_v[:, 0:1, :]).then_inc(x_first, 16)
            load_chunk(sp, 0)
            load_chunk(sp, 1)
            sp.dma_start(x[:, 1:G, :], u_v[:, 1:G, :]).then_inc(x_in[0], 16)
            for c in range(2, 1 + E):
                load_chunk(sp, c)
            params = [(cw[:], conv_w), (cb[:], conv_b), (nw[:], norm_w),
                      (bias8[:], dt_bias.partition_broadcast(P)), (alog8[:], a_log.partition_broadcast(P)),
                      (d8[:], d_param.partition_broadcast(P))]
            for to, of in params:
                sp.dma_start(to, of).then_inc(par_in, 16)
            for i in range(1, NG):
                sp.dma_start(x[:, G * i:G * i + G, :], u_v[:, G * i:G * i + G, :]).then_inc(x_in[i], 16)
            for c in range(LATE, len(chunks)):
                load_chunk(sp, c)
            with sp.Fori(0, T) as t:
                sp.wait_ge(FFN[1].added, t + 1)
                sp.dma_start(out_v[:, bass.ds(t, 1), :], x[:, bass.ds(t, 1), :]).then_inc(stored, 16)
            sp.wait_ge(stored, 16 * T)

        @block.gpsimd
        def _(pool):
            pool.memset(ident[:], 0.0).then_inc(const_done, 1)
            pool.memset(upto[:], 0.0).then_inc(const_done, 1)
            pool.memset(below[:], 0.0).then_inc(const_done, 1)
            pool.memset(half_neg[:], -0.5).then_inc(const_done, 1)
            pool.wait_ge(const_done, 4)
            pool.affine_select(out=ident[:], in_=ident[:], compare_op=ALU.not_equal, fill=1.0, base=0,
                               pattern=[[-1, P]], channel_multiplier=1).then_inc(const_done, 1)
            pool.affine_select(out=upto[:], in_=upto[:], compare_op=ALU.is_gt, fill=1.0, base=0,
                               pattern=[[-1, P]], channel_multiplier=1).then_inc(const_done, 1)
            pool.affine_select(out=below[:], in_=below[:], compare_op=ALU.is_ge, fill=1.0, base=0,
                               pattern=[[1, P]], channel_multiplier=-1).then_inc(const_done, 1)
            pool.iota(iota8[:], pattern=[[1, E]], base=0, channel_multiplier=0,
                      allow_small_or_imprecise_dtypes=True).then_inc(const_done, 1)

            def root(F, t, s):
                pool.wait_ge(F.var, t + 1)
                pool.tensor_tensor(rstd[:, s:s + 1], ve[:, s:s + 1], half_neg[:, 0:1], ALU.pow).then_inc(F.rstd, 1)

            def copy(to, of):
                return pool.tensor_scalar(to, of, 1.0, 0.0, ALU.mult, ALU.add)

            def split_w2(e):
                raw = raw2[e % NSLOT]
                landed(pool, e)
                copy(w2h[:, e, :], raw).then_inc(w2_split, 1)
                pool.wait_ge(w2_split, 2 * e + 1)
                pool.tensor_tensor(w2l[:, e, :], raw, as_f32(w2h[:, e, :]), ALU.subtract).then_inc(w2_split, 1)

            def split_late(c):
                kind, _, c0, n = chunks[c]
                raw = raw1[c % NSLOT][:, :, 0:n]
                landed(pool, c)
                if kind == "in":
                    hi, lo = wih[:, :, c0:c0 + n], wil[:, :, c0:c0 + n]
                else:
                    hi, lo = woh[:, c0:c0 + KD, :], wol[:, c0:c0 + KD, :]
                    pool.wait_ge(par_in, 96)
                    for k in range(KD):
                        ins = pool.tensor_scalar(raw[:, k, :], raw[:, k, :], nw[:, c0 + k:c0 + k + 1], 0.0, ALU.mult,
                                                 ALU.add)
                    ins.then_inc(scaled, 1)
                    pool.wait_ge(scaled, c0 // KD + 1)
                copy(hi, raw).then_inc(late_split, 1)
                pool.wait_ge(late_split, 2 * (c - LATE) + 1)
                pool.tensor_tensor(lo, raw, as_f32(hi), ALU.subtract).then_inc(late_split, 1)

            def group_root(g):
                pool.wait_ge(S.stats, 2 * G * (g + 1))
                pool.tensor_scalar(gve[:], gmv[:, :, 1], EPS, None, ALU.add).then_inc(S.var, 1)
                pool.wait_ge(S.var, g + 1)
                pool.tensor_tensor(grstd[:], gve[:], half_neg[:], ALU.pow).then_inc(S.rstd, 1)

            root(FFN[0], 0, 0)
            split_w2(0)
            root(FFN[0], 1, 1)
            for e in range(1, 1 + E):
                split_w2(e)
            for t in range(2, T):
                if t >= T - 2:
                    group_root(t - T + 2)
                root(FFN[0], t, t % 2)
                if LATE + t - 2 < len(chunks):
                    split_late(LATE + t - 2)

            def decay(t):
                g, j = divmod(t, G)
                pool.wait_ge(S.dA, 2 * (g + 1))
                if t:
                    pool.wait_ge(S.seg, t)
                for r, a in ((rh, dAh), (rl, dAl)):
                    pool.tensor_tensor(r[:], upto[:].unsqueeze(1).broadcast_to([P, H, P]),
                                       as_f32(a[:, g % 2, j, :]).unsqueeze(2).broadcast_to([P, H, P]),
                                       ALU.mult).then_inc(S.decay, 1)

            def gate(t):
                g, j = divmod(t, G)
                pool.wait_ge(S.y, t + 1)
                pool.wait_ge(S.zs, t + 1)
                pool.wait_ge(S.z0_silu, g + 1)
                if t % 2:
                    pool.wait_ge(S.off, t // 2 + 1)
                    pool.tensor_tensor(y, y, off, ALU.add).then_inc(S.yoff, 1)
                    pool.wait_ge(S.yoff, t // 2 + 1)
                if t >= 2:
                    pool.wait_ge(S.yT, t - 1)
                    pool.wait_ge(S.sumsq, t - 1)
                pool.tensor_tensor(yz[:, t % 2, :], y, zs[:, g % 2, j, :], ALU.mult).then_inc(S.yz, 1)

            def norm_root(t):
                pool.wait_ge(S.sumsq, t + 1)
                pool.tensor_scalar(vy[:, t % 2:t % 2 + 1], ss[:, t % 2:t % 2 + 1], 1.0 / DI, EPS,
                                   ALU.mult, ALU.add).then_inc(S.vy, 1)
                pool.wait_ge(S.vy, t + 1)
                if t >= 2:
                    pool.wait_ge(S.added, t - 1)
                pool.tensor_tensor(ry[:, t % 2:t % 2 + 1], vy[:, t % 2:t % 2 + 1], half_neg[:, 0:1],
                                   ALU.pow).then_inc(S.ry, 1)

            def scaled_inputs(t):
                pool.wait_ge(S.dtx, t + 1)
                pool.wait_ge(S.edec, t + 1)
                if t >= 2:
                    pool.wait_ge(S.carry, t // 2)
                pool.tensor_tensor(dtxe.rearrange("p (h d) -> p h d", h=H),
                                   dtx[:, t % 2, :].rearrange("p (h d) -> p h d", h=H),
                                   edec[:, t % 4, :].unsqueeze(2).broadcast_to([P, H, HD]),
                                   ALU.mult).then_inc(S.dtxe, 1)

            decay(0)
            for n in range(-3, T + 6):
                g, j = divmod(n, G)
                if j == 0:
                    of_tile(gate, n - 5)
                    of_tile(scaled_inputs, n - 4)
                    of_tile(decay, n - 2, first=1)
                    of_tile(gate, n - 4)
                    of_tile(norm_root, n - 5)
                elif j == 1:
                    of_tile(decay, n - 2, first=1)
                    of_tile(norm_root, n - 5)
                    if n == T + 1:
                        for k in range(2):
                            root(FFN[1], k, k)
                    of_tile(gate, n - 4)
                elif j == 2:
                    of_tile(scaled_inputs, n - 4)
                    of_tile(decay, n - 2, first=1)
                else:
                    of_tile(norm_root, n - 6)
                    of_tile(gate, n - 5)
                    of_group(group_root, g + 2, first=2)
                    of_tile(decay, n - 2, first=1)
                    of_tile(norm_root, n - 5)

            with pool.Fori(1, T // 2) as i:
                for s in range(2):
                    root(FFN[1], 2 * i + s, s)

        @block.scalar
        def _(act):
            for k in range(1, KD):
                load_shared(act, k)

            def split_hi(e):
                landed(act, e)
                _, _, c0, n = chunks[e]
                act.activation(w1h[:, :, c0:c0 + n], raw1[e % NSLOT][:, :, 0:n], ACT.Copy).then_inc(w1_hi, 1)

            def x_hi(F, t, s):
                act.wait_ge(F.xT, t + 1)
                act.activation(xTh[:, s], bank[x_bank(F, t)][:, 0:D].rearrange("p (k n) -> p k n", k=KD),
                               ACT.Copy).then_inc(F.xhi, 1)

            def silu(F, q, r, t, s, e):
                act.wait_ge(F.gate_up, count(q))
                if not isinstance(q, int) or q >= 3:
                    act.wait_ge(F.hidden, count(q - 3))
                if e == SH:
                    act.activation(sil[:, r % 3, :], bank[1 + r % 3][:, 0:I], ACT.Silu).then_inc(F.silu, 1)
                else:
                    act.wait_ge(F.prob, t + 1)
                    act.activation(sil[:, r % 3, :], bank[1 + r % 3][:, 0:I], ACT.Silu,
                                   scale=prob[:, s, e:e + 1]).then_inc(F.silu, 1)

            def h_hi(F, q, r):
                act.wait_ge(F.hT, count(q))
                if not isinstance(q, int) or q >= 3:
                    act.wait_ge(F.down, count(q - 3))
                act.activation(hTh[:, r % 3, :], bank[4 - 4 * (r % 2)][:, 0:P], ACT.Copy).then_inc(F.hhi, 1)

            def tanh_logits(F, t, s):
                act.wait_ge(F.logits, t + 1)
                act.activation(th8[:], lg[:, s, :], ACT.Tanh, scale=0.5).then_inc(F.tanh, 1)

            def first_step(F):
                silu(F, 0, 0, 0, 0, SH)
                tanh_logits(F, 0, 0)
                if F is FFN[0]:
                    split_hi(2)
                h_hi(F, 0, 0)

            def ffn(F, beside):
                def tile(t, s):
                    q0 = t * NSTEP + BEFORE
                    for j, e in enumerate(ORDER):
                        q, r = q0 + j, s * NSTEP + BEFORE + j
                        last = isinstance(t, int) and t == T - 1
                        if F is FFN[0] and isinstance(t, int) and t == 0 and e != SH and e + 3 <= E:
                            split_hi(e + 3)
                        if not (last and e == SH):
                            silu(F, q, r, t, s, e)
                        if not isinstance(q, int) or real(q - TURN):
                            h_hi(F, q - TURN, r - TURN)
                        if j == 2 and not last:
                            x_hi(F, t + 1, 1 - s)
                        if e == SH and not last:
                            tanh_logits(F, t + 1, 1 - s)
                        if isinstance(t, int):
                            beside(t, j)

                for s in range(2):
                    tile(s, s)
                with act.Fori(1, T // 2 - 2) as i:
                    for s in range(2):
                        tile(2 * i + s, s)
                for t in range(T - 4, T):
                    tile(t, t % 2)
                for q in (LAST - 1, LAST):
                    h_hi(F, q, q - NSTEP * (T - 2))

            def n_hi(g, pair):
                act.wait_ge(S.nT, 2 * g + pair + 1)
                if g:
                    act.wait_ge(S.conv, NC * g)
                    act.wait_ge(S.z0, G * g)
                    act.wait_ge(S.z1, G * g)
                src = bank[piece_bank(g, f"n{pair}")][:].rearrange("p (k n) -> p k n", k=KD)
                act.activation(nTh[:, :, pair * 2 * P:(pair + 1) * 2 * P], src, ACT.Copy).then_inc(S.nhi, 1)

            def conv_out(g, k):
                c = CONV_ORDER[k]
                return xc[:, g % 2, c, :] if c < KI else bc[:]

            def conv_last(g, k):
                i = NC * g + k
                c = CONV_ORDER[k]
                act.wait_ge(S.conv, i + 1)
                if g and c >= KI:
                    act.wait_ge(S.xc, NC * g)
                if g >= 2 and c < KI:
                    act.wait_ge(S.xtok, G * (g - 1))
                act.activation(conv_out(g, k), bank[piece_bank(g, f"c{k}")][:], ACT.Identity, scale=cw[:, c, TAPS - 1:TAPS],
                               bias=cb[:, c:c + 1]).then_inc(S.acc, 1)

            def conv_silu(g, k):
                i = NC * g + k
                act.wait_ge(S.tap, (TAPS - 1) * (i + 1))
                if CONV_ORDER[k] < KI:
                    act.activation(conv_out(g, k), conv_out(g, k), ACT.Silu).then_inc(S.xc, 1)
                    return
                if g >= 2:
                    act.wait_ge(S.carry, G * (g - 1) // 2)
                    act.wait_ge(S.off_mm, G * (g - 1) // 2)
                    act.wait_ge(S.misc, G * (g - 1))
                act.activation(BT[:, g % 2, :], bc[0:N, :], ACT.Silu)
                act.activation(CT[:, g % 2, :], bc[N:P, :], ACT.Silu).then_inc(S.xc, 1)

            def z0_out(g, j):
                i = G * g + j
                b = bank[piece_bank(g, f"z0{j}")]
                act.wait_ge(S.z0, i + 1)
                if j == 0 and g:
                    act.wait_ge(S.dt, DT_OPS * (g - 1) + 1)
                if g >= 2:
                    act.wait_ge(S.yz, G * (g - 1))
                act.activation(dtr[:, j, :], b[:, D:ZC], ACT.Copy)
                act.activation(zs[:, g % 2, j, 0:D], b[:, 0:D], ACT.Copy).then_inc(S.z0_out, 1)

            def z0_silu(g):
                act.wait_ge(S.z0_out, G * (g + 1))
                z = zs[:, g % 2, :, 0:D]
                act.activation(z, z, ACT.Silu).then_inc(S.z0_silu, 1)

            def z1_silu(g, j):
                i = G * g + j
                act.wait_ge(S.z1, i + 1)
                if g >= 2:
                    act.wait_ge(S.yz, G * (g - 1))
                act.activation(zs[:, g % 2, j, D:DI], bank[piece_bank(g, f"z1{j}")][:, 0:D], ACT.Silu).then_inc(S.zs, 1)

            def dt_exp(g):
                act.wait_ge(S.dt, DT_OPS * g + 2)
                act.activation(dtu[:], dtn[:], ACT.Exp).then_inc(S.dt_exp, 1)
                if g == 0:
                    act.wait_ge(par_in, 96)
                    act.activation(a8[:], alog8[:], ACT.Exp).then_inc(a8_done, 1)

            def decays(t):
                act.wait_ge(S.seg, t + 1)
                if t >= 2:
                    act.wait_ge(S.y_mm, t - 1)
                for half in range(2):
                    act.activation(M[:, t % 2, half * 4:half * 4 + 4, :], bank[half][:].rearrange("p (h n) -> p h n", h=4),
                                   ACT.Exp).then_inc(S.exp, 1)

            def decay_out(t):
                act.wait_ge(S.dec, t + 1)
                if t >= 4:
                    act.wait_ge(S.dtxe, t // 2 - 1)
                    act.wait_ge(S.off, t // 2 - 1)
                act.activation(edec[:, t % 4, :], bank[3][:, P:P + H], ACT.Exp).then_inc(S.edec, 1)

            def carried(t):
                act.wait_ge(S.carry, t // 2 + 1)
                if t:
                    act.wait_ge(S.off_mm, t // 2)
                act.activation(state[:], bank[7][0:N, :], ACT.Copy).then_inc(S.state, 1)

            def square(t):
                act.wait_ge(S.yz, t + 1)
                if t >= 2:
                    act.wait_ge(S.vy, t - 1)
                if t:
                    act.wait_ge(S.sumsq, t)
                act.activation(sq, yz[:, t % 2, :], ACT.Square, accum_out=ss[:, t % 2:t % 2 + 1]).then_inc(S.sumsq, 1)

            def y_hi(t):
                act.wait_ge(S.yT, t + 1)
                if t:
                    act.wait_ge(S.o, t)
                act.activation(yTh[:], bank[turned_bank(t)][:].rearrange("p (k n) -> p k n", k=KI), ACT.Copy).then_inc(S.yhi, 1)

            def first_group(t, j):
                if t == T - 4 and j in (5, 7):
                    n_hi(0, (j - 5) // 2)
                if t == T - 3 and 4 <= j < 8:
                    z0_out(0, j - 4)
                if t == T - 2 and j == 1:
                    dt_exp(0)
                if t == T - 2 and j == 5:
                    conv_last(0, 0)
                if t == T - 1 and j in (1, 5, 7):
                    conv_last(0, j // 3 + 1)

            def last_tile(t, j):
                if t == 0 and j == 0:
                    square(T - 1)
                if t == 0 and j == 3:
                    y_hi(T - 1)

            x_hi(FFN[0], 0, 0)
            split_hi(0)
            split_hi(1)
            first_step(FFN[0])
            ffn(FFN[0], first_group)

            decays(0)
            decay_out(0)
            conv_last(0, 4)
            for k in range(G):
                conv_silu(0, k)
                z1_silu(0, k)
            conv_silu(0, NC - 1)
            z0_silu(0)
            for n in range(-3, T + 6):
                g, j = divmod(n, G)
                if j == 0:
                    of_tile(decays, n + 1, first=1)
                    of_group(z0_out, g + 1, 2)
                    of_tile(y_hi, n - 1, last=T - 2)
                    of_group(z0_out, g + 1, 3)
                    of_tile(square, n - 1, last=T - 2)
                    of_tile(decay_out, n + 1, first=1)
                    of_group(dt_exp, g + 1)
                    of_group(conv_last, g + 1, 0)
                    of_group(conv_last, g + 1, 1)
                    of_tile(carried, n)
                elif j == 1:
                    of_tile(decays, n + 1, first=1)
                    of_group(conv_silu, g + 1, 0)
                    of_group(conv_silu, g + 1, 1)
                    of_tile(y_hi, n - 1, last=T - 2)
                    of_group(z1_silu, g + 1, 0)
                    of_tile(decay_out, n + 1, first=1)
                    of_group(conv_last, g + 1, 2)
                    of_tile(square, n - 1, last=T - 2)
                elif j == 2:
                    of_group(conv_last, g + 1, 3)
                    of_tile(decay_out, n + 1, first=1)
                    of_tile(decays, n + 1, first=1)
                    of_group(conv_silu, g + 1, 2)
                    of_group(conv_last, g + 1, 4)
                    of_tile(y_hi, n - 1, last=T - 2)
                    of_tile(square, n - 1, last=T - 2)
                    of_group(z1_silu, g + 1, 1)
                    of_group(conv_silu, g + 1, 3)
                else:
                    of_group(conv_silu, g + 1, 4)
                    of_group(z1_silu, g + 1, 2)
                    of_group(z1_silu, g + 1, 3)
                    of_tile(carried, n - 1)
                    of_group(z0_silu, g + 1)
                    of_group(n_hi, g + 2, 0)
                    of_group(n_hi, g + 2, 1)
                    of_tile(decay_out, n + 1, first=1)
                    of_tile(decays, n + 1, first=1)
                    of_tile(square, n - 1, last=T - 2)
                    if n == T - 1:
                        x_hi(FFN[1], 0, 0)
                    of_tile(y_hi, n - 1, last=T - 2)
                    of_group(z0_out, g + 2, 0)
                    of_group(z0_out, g + 2, 1)

            first_step(FFN[1])
            ffn(FFN[1], last_tile)

        @block.vector
        def _(dve):
            def split_lo(e):
                _, _, c0, n = chunks[e]
                dve.wait_ge(w1_hi, e + 1)
                dve.tensor_tensor(w1l[:, :, c0:c0 + n], raw1[e % NSLOT][:, :, 0:n], as_f32(w1h[:, :, c0:c0 + n]),
                                  ALU.subtract).then_inc(w1_lo, 1)

            def stats(F, t, s, ready):
                ready(t)
                dve.bn_stats(st6[:, s, :], x[:, bass.ds(t, 1), :].squeeze(1) if not isinstance(t, int) else x[:, t, :]).then_inc(F.stats, 1)
                dve.drain()
                dve.bn_aggr(mv[:, s, :], st6[:, s, :]).then_inc(F.stats, 1)
                dve.wait_ge(F.stats, 2 * t + 2)
                dve.tensor_scalar(ve[:, s:s + 1], mv[:, s, 1:2], EPS, None, ALU.add).then_inc(F.var, 1)

            def normal(F, t, s):
                dve.wait_ge(F.rstd, t + 1)
                if not isinstance(t, int) or t >= 2:
                    dve.wait_ge(F.xT, t - 1)
                src = x[:, bass.ds(t, 1), :].squeeze(1) if not isinstance(t, int) else x[:, t, :]
                dve.tensor_scalar(xn[:, s, :], src, mv[:, s, 0:1], rstd[:, s:s + 1], ALU.subtract,
                                  ALU.mult).then_inc(F.xn, 1)

            def x_lo(F, t, s):
                dve.wait_ge(F.xhi, t + 1)
                dve.tensor_tensor(xTl[:, s], bank[x_bank(F, t)][:, 0:D].rearrange("p (k n) -> p k n", k=KD), as_f32(xTh[:, s]),
                                  ALU.subtract).then_inc(F.xlo, 1)

            def hidden(F, q, r, s, e):
                dve.wait_ge(F.silu, count(q))
                if not isinstance(q, int) or q >= 3:
                    dve.wait_ge(F.hT, count(q - 3))
                if e == SH:
                    dve.tensor_copy(lg[:, s, :], bank[1 + r % 3][:, CG:CG + E]).then_inc(F.logits, 1)
                    dve.tensor_tensor(hid[:, r % 3, :], bank[1 + r % 3][:, I:CG], sil[:, r % 3, :],
                                      ALU.mult).then_inc(F.hidden, 1)
                else:
                    dve.scalar_tensor_tensor(out=hid[:, r % 3, :], in0=bank[1 + r % 3][:, I:CG], scalar=prob[:, s, e:e + 1],
                                             in1=sil[:, r % 3, :], op0=ALU.mult, op1=ALU.mult).then_inc(F.hidden, 1)

            def h_lo(F, q, r):
                dve.wait_ge(F.hhi, count(q))
                dve.tensor_tensor(hTl[:, r % 3, :], bank[4 - 4 * (r % 2)][:, 0:P], as_f32(hTh[:, r % 3, :]),
                                  ALU.subtract).then_inc(F.hlo, 1)

            def route(F, t, s):
                n = 5 * t
                dve.drain()
                dve.max(top[:], lg[:, s, :]).then_inc(F.route, 1)
                dve.drain()
                dve.max_index(topi[:], top[:], lg[:, s, :]).then_inc(F.route, 1)
                dve.wait_ge(F.route, n + 2)
                dve.tensor_copy(topf[:], topi[:, 0:2]).then_inc(F.route, 1)
                dve.wait_ge(F.route, n + 3)
                dve.tensor_scalar(one1[:], iota8[:], topf[:, 0:1], None, ALU.is_equal).then_inc(F.route, 1)
                dve.wait_ge(F.route, n + 4)
                dve.scalar_tensor_tensor(out=one2[:], in0=iota8[:], scalar=topf[:, 1:2], in1=one1[:],
                                         op0=ALU.is_equal, op1=ALU.add).then_inc(F.route, 1)

            def shares(F, t, s):
                dve.wait_ge(F.tanh, t + 1)
                dve.wait_ge(F.route, 5 * t + 5)
                dve.scalar_tensor_tensor(out=p2[:], in0=th8[:], scalar=1.0, in1=one2[:], op0=ALU.add,
                                         op1=ALU.mult).then_inc(share_step, 1)
                dve.wait_ge(share_step, t + 1 + (0 if F is FFN[0] else T))
                dve.tensor_scalar(prob[:, s, :], p2[:], 0.5, None, ALU.mult).then_inc(F.prob, 1)

            def add_out(F, t, s):
                q = (t + 1) * NSTEP + BEFORE - 1
                dve.wait_ge(F.down, count(q))
                to = x[:, t, :] if isinstance(t, int) else x[:, bass.ds(t, 1), :].squeeze(1)
                dve.scalar_tensor_tensor(out=to, in0=bank[5 + s][:, 0:D], scalar=0.5, in1=to, op0=ALU.mult,
                                         op1=ALU.add).then_inc(F.added, 1)

            def ffn(F, ready, beside):
                def tile(t, s):
                    q0 = t * NSTEP + BEFORE
                    last = isinstance(t, int) and t == T - 1
                    for j, e in enumerate(ORDER):
                        q, r = q0 + j, s * NSTEP + BEFORE + j
                        if F is FFN[0] and isinstance(t, int) and t == 0 and e != SH and e + 3 <= E:
                            split_lo(e + 3)
                        if j == 0 and not last:
                            normal(F, t + 1, 1 - s)
                        if not (last and e == SH):
                            hidden(F, q, r, s if e != SH else 1 - s, e)
                        if not isinstance(q, int) or real(q - TURN):
                            h_lo(F, q - TURN, r - TURN)
                        if j == 2 and not last:
                            x_lo(F, t + 1, 1 - s)
                        if j == 4 and not (isinstance(t, int) and t == 0):
                            add_out(F, t - 1, 1 - s)
                        if e == SH and not last:
                            route(F, t + 1, 1 - s)
                        if j == AT_SH + 1 and not last:
                            shares(F, t + 1, 1 - s)
                        if j == 7 and not (isinstance(t, int) and t >= T - 2):
                            stats(F, t + 2, s, ready)
                        if isinstance(t, int):
                            beside(t, j)

                for s in range(2):
                    tile(s, s)
                with dve.Fori(1, T // 2 - 2) as i:
                    for s in range(2):
                        tile(2 * i + s, s)
                for t in range(T - 4, T):
                    tile(t, t % 2)
                for q in (LAST - 1, LAST):
                    h_lo(F, q, q - NSTEP * (T - 2))
                add_out(F, T - 1, 1)

            dve.wait_ge(const_done, 8)
            dve.tensor_copy(below_r[:], below[:]).then_inc(const_done, 1)

            def first_ready(t):
                if isinstance(t, int) and t == 0:
                    dve.wait_ge(x_first, 16)
                if isinstance(t, int) and t == 1:
                    dve.wait_ge(x_in[0], 16)
                if isinstance(t, int) and t == 2:
                    for i in range(1, NG):
                        dve.wait_ge(x_in[i], 16)

            def g_stats(g):
                for j in range(G):
                    dve.wait_ge(FFN[0].added, G * g + j + 1)
                    if g:
                        dve.wait_ge(S.xn, G * g)
                    dve.bn_stats(gst[:, j, :], x[:, G * g + j, :]).then_inc(S.stats, 1)
                for j in range(G):
                    dve.wait_ge(S.stats, 2 * G * g + G)
                    dve.bn_aggr(gmv[:, j, :], gst[:, j, :]).then_inc(S.stats, 1)

            def g_normal(g):
                dve.wait_ge(S.rstd, g + 1)
                if g:
                    dve.wait_ge(S.nT, 2 * g)
                for j in range(G):
                    dve.tensor_scalar(gxn[:, j, :], x[:, G * g + j, :], gmv[:, j, 0:1], grstd[:, j:j + 1],
                                      ALU.subtract, ALU.mult).then_inc(S.xn, 1)

            def n_lo(g, pair):
                dve.wait_ge(S.nhi, 2 * g + pair + 1)
                cols = slice(pair * 2 * P, (pair + 1) * 2 * P)
                dve.tensor_tensor(nTl[:, :, cols], bank[piece_bank(g, f"n{pair}")][:].rearrange("p (k n) -> p k n", k=KD),
                                  as_f32(nTh[:, :, cols]), ALU.subtract).then_inc(S.nlo, 1)

            def dt_steps(g, first, last):
                gp = g % 2
                a8_all = a8[:].unsqueeze(1).broadcast_to([P, G, H])
                for k in range(first, last):
                    if k and k <= DT_OPS:
                        dve.wait_ge(S.dt, DT_OPS * g + k)
                    if k == 0:
                        dve.wait_ge(S.z0_out, G * (g + 1))
                        dve.wait_ge(par_in, 96)
                        ins = dve.tensor_tensor(dtv[:], dtr[:], bias8[:].unsqueeze(1).broadcast_to([P, G, H]), ALU.add)
                    elif k == 1:
                        ins = dve.scalar_tensor_tensor(out=dtn[:], in0=dtv[:], scalar=-1.0, in1=dtv[:], op0=ALU.mult, op1=ALU.min)
                    elif k == 2:
                        dve.wait_ge(S.dt_exp, g + 1)
                        ins = dve.tensor_scalar(dtd[:], dtu[:], 2.0, None, ALU.add)
                    elif k == 3:
                        ins = dve.reciprocal(dtd[:], dtd[:])
                    elif k == 4:
                        ins = dve.tensor_tensor(dts[:], dtu[:], dtd[:], ALU.mult)
                    elif k == 5:
                        ins = dve.tensor_tensor(dts2[:], dts[:], dts[:], ALU.mult)
                    elif k == 6:
                        ins = dve.tensor_scalar(dtq[:], dts2[:], ATANH[0], None, ALU.mult)
                    elif k < 6 + len(ATANH):
                        ins = dve.scalar_tensor_tensor(out=dtq[:], in0=dtq[:], scalar=ATANH[k - 6], in1=dts2[:], op0=ALU.add,
                                                       op1=ALU.mult)
                    elif k == DT_OPS - 4:
                        ins = dve.scalar_tensor_tensor(out=dtq[:], in0=dtq[:], scalar=1.0, in1=dts[:], op0=ALU.add, op1=ALU.mult)
                    elif k == DT_OPS - 3:
                        ins = dve.tensor_scalar(dtv[:], dtv[:], 0.0, None, ALU.max)
                    elif k == DT_OPS - 2:
                        if g >= 2:
                            dve.wait_ge(S.dec, G * (g - 1))
                            dve.wait_ge(S.decay, 2 * G * (g - 1))
                        ins = dve.scalar_tensor_tensor(out=dt[:, gp], in0=dtq[:], scalar=2.0, in1=dtv[:], op0=ALU.mult, op1=ALU.add)
                    elif k == DT_OPS - 1:
                        dve.wait_ge(a8_done, 1)
                        ins = dve.scalar_tensor_tensor(out=dA[:, gp], in0=dt[:, gp], scalar=-1.0, in1=a8_all, op0=ALU.mult,
                                                       op1=ALU.mult)
                    elif k == DT_OPS:
                        dve.tensor_copy(dAh[:, gp], dA[:, gp]).then_inc(S.dA, 1)
                        continue
                    else:
                        dve.wait_ge(S.dA, 2 * g + 1)
                        dve.tensor_tensor(dAl[:, gp], dA[:, gp], as_f32(dAh[:, gp]), ALU.subtract).then_inc(S.dA, 1)
                        continue
                    ins.then_inc(S.dt, 1)

            def dt_first(g):
                dt_steps(g, 0, 2)

            def dt_part(g, k):
                dt_steps(g, 2 + 4 * k, 6 + 4 * k if k < 3 else DT_OPS + 2)

            def tap(g, k, s):
                i = NC * g + k
                c = CONV_ORDER[k]
                n = (TAPS - 1) * i + s
                if s == 1:
                    dve.wait_ge(S.acc, i + 1)
                else:
                    dve.wait_ge(S.tap, n - 1)
                a = (xc[:, g % 2, c, :] if c < KI else bc[:]).rearrange("p (b l) -> p b l", l=SEQ)
                r = bank[piece_bank(g, f"c{k}")][:].rearrange("p (b l) -> p b l", l=SEQ)
                dve.scalar_tensor_tensor(out=a[:, :, s:SEQ], in0=r[:, :, 0:SEQ - s], scalar=cw[:, c, TAPS - 1 - s:TAPS - s],
                                         in1=a[:, :, s:SEQ], op0=ALU.mult, op1=ALU.add).then_inc(S.tap, 1)

            def conv(g, k):
                for s in range(1, TAPS):
                    tap(g, k, s)

            def heads(ap):
                return ap.rearrange("p (h d) -> p h d", h=H)

            def masked(t):
                dve.wait_ge(S.misc, t + 1)
                if t:
                    dve.wait_ge(S.M, 2 * t)
                dve.tensor_tensor(cbm[:], bank[3][:, 0:P], upto[:], ALU.mult).then_inc(S.cbm, 1)
                if t % 2 == 0:
                    if t:
                        dve.wait_ge(S.carry, t // 2)
                    dve.tensor_copy(Btok[:], bank[3][:, 256:256 + N]).then_inc(S.btok, 1)

            def mixing(t):
                dve.wait_ge(S.cbm, t + 1)
                if t >= 2:
                    dve.wait_ge(S.y_mm, t - 1)
                for half in range(2):
                    dve.wait_ge(S.exp, 2 * t + half + 1)
                    hs = slice(4 * half, 4 * half + 4)
                    dve.tensor_tensor(M[:, t % 2, hs, :], M[:, t % 2, hs, :], cbm[:].unsqueeze(1).broadcast_to([P, 4, P]),
                                      ALU.mult).then_inc(S.M, 1)

            def scaled_x(t):
                g, j = divmod(t, G)
                dve.wait_ge(S.xtok, t + 1)
                dve.wait_ge(S.dt, DT_OPS * (g + 1))
                if t >= 2:
                    dve.wait_ge(S.y_mm, t - 1)
                if t >= 2 and t % 2 == 0:
                    dve.wait_ge(S.dtxe, t // 2)
                dve.tensor_tensor(heads(dtx[:, t % 2, :]), heads(bank[2][:]),
                                  dt[:, g % 2, j, :].unsqueeze(2).broadcast_to([P, H, HD]), ALU.mult).then_inc(S.dtx, 1)

            def skip(t):
                dve.wait_ge(S.xtok, t + 1)
                if t >= 2:
                    dve.wait_ge(S.y, t - 1)
                dve.tensor_tensor(heads(xD[:, t % 2, :]), heads(bank[2][:]),
                                  d8[:].unsqueeze(2).broadcast_to([P, H, HD]), ALU.mult).then_inc(S.xD, 1)

            def sum_y(t):
                dve.wait_ge(S.y_mm, t + 1)
                dve.wait_ge(S.xD, t + 1)
                if t:
                    dve.wait_ge(S.yz, t)
                dve.tensor_tensor(y, bank[4][:], xD[:, t % 2, :], ALU.add).then_inc(S.y, 1)
                if t % 2:
                    dve.wait_ge(S.off_mm, t // 2 + 1)
                    dve.wait_ge(S.edec, t + 1)
                    dve.tensor_tensor(heads(off), heads(bank[7][:]), edec[:, t % 4, :].unsqueeze(2).broadcast_to([P, H, HD]),
                                      ALU.mult).then_inc(S.off, 1)

            def y_lo(t):
                dve.wait_ge(S.yhi, t + 1)
                dve.tensor_tensor(yTl[:], bank[turned_bank(t)][:].rearrange("p (k n) -> p k n", k=KI), as_f32(yTh[:]),
                                  ALU.subtract).then_inc(S.ylo, 1)

            def add_ssd(t):
                dve.wait_ge(S.o, t + 1)
                dve.wait_ge(S.ry, t + 1)
                dve.scalar_tensor_tensor(out=x[:, t, :], in0=bank[out_bank(t)][:, 0:D], scalar=ry[:, t % 2:t % 2 + 1], in1=x[:, t, :],
                                         op0=ALU.mult, op1=ALU.add).then_inc(S.added, 1)

            def first_group(t, j):
                if t == T - 4 and j == 0:
                    g_stats(0)
                if t == T - 4 and j == 4:
                    g_normal(0)
                if t == T - 4 and j in (6, 8):
                    n_lo(0, j // 2 - 3)
                if t == T - 3 and j == 4:
                    g_stats(1)
                if t == T - 3 and j == 7:
                    g_normal(1)
                if t == T - 2 and j == 0:
                    dt_steps(0, 0, 2)
                if t == T - 2 and 2 <= j < 8:
                    dt_steps(0, 3 * j - 4, min(3 * j - 1, DT_OPS + 2))
                if t == T - 2 and j >= 6:
                    tap(0, 0, j - 5)
                if t == T - 1 and 2 <= j < 5:
                    tap(0, 1, j - 1)
                if t == T - 1 and j >= 6:
                    tap(0, 2, j - 5)

            def second_ready(t):
                dve.wait_ge(S.added, t + 1)

            def last_tile(t, j):
                if t == 0 and j == 3:
                    y_lo(T - 1)
                if t == 0 and j == 6:
                    add_ssd(T - 1)

            stats(FFN[0], 0, 0, first_ready)
            normal(FFN[0], 0, 0)
            x_lo(FFN[0], 0, 0)
            split_lo(0)
            stats(FFN[0], 1, 1, first_ready)
            split_lo(1)
            hidden(FFN[0], 0, 0, 0, SH)
            split_lo(2)
            route(FFN[0], 0, 0)
            h_lo(FFN[0], 0, 0)
            shares(FFN[0], 0, 0)
            ffn(FFN[0], first_ready, first_group)

            conv(0, 3)
            conv(0, 4)
            for n in range(-3, T + 6):
                g, j = divmod(n, G)
                if j == 0:
                    of_tile(scaled_x, n - 1)
                    of_tile(masked, n - 1)
                    of_tile(y_lo, n - 3, last=T - 2)
                    of_tile(sum_y, n - 2)
                    of_group(g_stats, g + 2, first=2)
                    if n == T:
                        dve.wait_ge(S.carry, T // 2)
                        normal(FFN[1], 0, 0)
                    of_tile(mixing, n - 1)
                    of_tile(scaled_x, n)
                    of_group(n_lo, g + 1, 0)
                    of_tile(add_ssd, n - 3, last=T - 2)
                    of_group(n_lo, g + 1, 1)
                    of_tile(skip, n)
                elif j == 1:
                    if n == T + 1:
                        x_lo(FFN[1], 0, 0)
                    of_tile(sum_y, n - 2)
                    of_tile(masked, n - 1)
                    of_tile(y_lo, n - 3, last=T - 2)
                    of_tile(mixing, n - 1)
                    of_tile(scaled_x, n)
                    of_tile(masked, n)
                    of_group(g_normal, g + 2, first=2)
                    of_tile(skip, n)
                    of_tile(add_ssd, n - 3, last=T - 2)
                    of_tile(mixing, n)
                    of_group(dt_first, g + 1)
                elif j == 2:
                    of_tile(y_lo, n - 3, last=T - 2)
                    of_group(dt_part, g + 1, 0)
                    of_tile(sum_y, n - 2)
                    of_group(dt_part, g + 1, 1)
                    of_tile(scaled_x, n)
                    of_group(conv, g + 1, 0)
                    if n == T - 2:
                        stats(FFN[1], 0, 0, second_ready)
                        stats(FFN[1], 1, 1, second_ready)
                    of_tile(masked, n)
                    of_group(conv, g + 1, 1)
                    of_tile(add_ssd, n - 3, last=T - 2)
                    of_tile(skip, n)
                    of_group(dt_part, g + 1, 2)
                    of_tile(mixing, n)
                    of_tile(y_lo, n - 2, last=T - 2)
                    of_tile(sum_y, n - 1)
                else:
                    of_group(conv, g + 1, 2)
                    of_group(conv, g + 1, 3)
                    of_tile(add_ssd, n - 3, last=T - 2)
                    of_group(dt_part, g + 1, 3)
                    of_group(conv, g + 1, 4)
                    of_tile(skip, n)

            hidden(FFN[1], 0, 0, 0, SH)
            route(FFN[1], 0, 0)
            h_lo(FFN[1], 0, 0)
            shares(FFN[1], 0, 0)
            ffn(FFN[1], second_ready, last_tile)

        @block.tensor
        def _(pe):
            def product(out_ap, lhs, rhs, first=True, last=True):
                pe.matmul(out_ap, lhs[0], rhs[0], start=first, stop=False)
                pe.matmul(out_ap, lhs[0], rhs[1], start=False, stop=False)
                return pe.matmul(out_ap, lhs[1], rhs[0], start=False, stop=last)

            def x_turn(F, t, s):
                pe.wait_ge(F.xn, t + 1)
                if not isinstance(t, int) or t >= 1:
                    pe.wait_ge(F.xlo, t)
                for k in range(KD):
                    ins = pe.transpose(bank[x_bank(F, t)][:, k * P:(k + 1) * P], xn[:, s, k * P:(k + 1) * P], ident[:])
                ins.then_inc(F.xT, 1)

            def gate_up(F, q, r, t, s, e):
                if not isinstance(q, int) or q >= 3:
                    pe.wait_ge(F.hidden, count(q - 3))
                pe.wait_ge(F.xlo, t + 1)
                if F is FFN[0] and isinstance(t, int) and t == 0:
                    pe.wait_ge(w1_lo, e + 2)
                c0, n = (0, CG + E) if e == SH else (CG + E + e * CG, CG)
                for k in range(KD):
                    ins = product(bank[1 + r % 3][:, 0:n], (xTh[:, s, k, :], xTl[:, s, k, :]),
                                  (w1h[:, k, c0:c0 + n], w1l[:, k, c0:c0 + n]), k == 0, k == KD - 1)
                ins.then_inc(F.gate_up, 1)

            def h_turn(F, q, r):
                pe.wait_ge(F.hidden, count(q))
                if not isinstance(q, int) or q >= 2:
                    pe.wait_ge(F.hlo, count(q - 2))
                pe.transpose(bank[4 - 4 * (r % 2)][:, 0:P], hid[:, r % 3, :], ident[:]).then_inc(F.hT, 1)

            def down(F, q, r, s, e, t):
                if F is FFN[0] and isinstance(t, int) and t == 0:
                    pe.wait_ge(w2_split, 2 * (e + 2))
                pe.wait_ge(F.hlo, count(q))
                if e == SH and (not isinstance(t, int) or t >= 2):
                    pe.wait_ge(F.added, t - 1)
                if F is FFN[1] and e == SH and isinstance(t, int) and t == 1:
                    pe.wait_ge(S.added, T)
                product(bank[5 + s][:, 0:D], (hTh[:, r % 3, :], hTl[:, r % 3, :]),
                        (w2h[:, e + 1, :], w2l[:, e + 1, :]), e == SH, e == E - 1).then_inc(F.down, 1)

            def ffn(F, beside):
                def tile(t, s):
                    q0 = t * NSTEP + BEFORE
                    last = isinstance(t, int) and t == T - 1
                    for j, e in enumerate(ORDER):
                        q, r = q0 + j, s * NSTEP + BEFORE + j
                        if j == 2 and not last:
                            if F is FFN[0] and isinstance(t, int) and t in (T - 3, T - 2):
                                pe.wait_ge(*[(S.nlo, 2), (S.z0_out, G)][t - T + 3])
                            if F is FFN[1] and isinstance(t, int) and t == 0:
                                pe.wait_ge(S.added, T - 1)
                            x_turn(F, t + 1, 1 - s)
                        if not (last and e == SH):
                            of = (t + 1, 1 - s) if e == SH else (t, s)
                            gate_up(F, q, r, *of, e)
                        if not isinstance(q, int) or real(q - TURN):
                            h_turn(F, q - TURN, r - TURN)
                        if not isinstance(q, int) or real(q - DOWN):
                            down_of(F, q - DOWN, r - DOWN, t, s, j - DOWN)
                        if isinstance(t, int):
                            beside(t, j)

                def down_of(F, q, r, t, s, j):
                    if j < 0:
                        e = ORDER[NSTEP + j]
                        down(F, q, r, s if e == SH else 1 - s, e, t if e == SH else t - 1)
                    else:
                        e = ORDER[j]
                        down(F, q, r, 1 - s if e == SH else s, e, t + 1 if e == SH else t)

                for s in range(2):
                    tile(s, s)
                with pe.Fori(1, T // 2 - 2) as i:
                    for s in range(2):
                        tile(2 * i + s, s)
                for t in range(T - 4, T):
                    tile(t, t % 2)
                for n in range(DOWN):
                    q = LAST + 1 + n
                    r = q - NSTEP * (T - 2)
                    if n < TURN:
                        h_turn(F, q - TURN, r - TURN)
                    if real(q - DOWN):
                        down_of(F, q - DOWN, r - DOWN, T - 1, 1, NSTEP - DOWN + n)

            ends = count(LAST)
            last_read = {0: (FFN[0].hlo, ends), 4: (FFN[0].hlo, ends), 5: (FFN[0].added, T - 1),
                         6: (FFN[0].added, T)}
            last_read.update({b: (FFN[0].hidden, ends) for b in (1, 2, 3)})

            def reuse(b, sem_, value):
                if b in last_read:
                    pe.wait_ge(*last_read[b])
                last_read[b] = (sem_, value)

            def n_turn(g, pair):
                b = piece_bank(g, f"n{pair}")
                reuse(b, S.nlo, 2 * g + pair + 1)
                pe.wait_ge(S.xn, G * g + 2 * pair + 2)
                for k in range(KD):
                    for v in range(2):
                        c = k * 2 * P + v * P
                        ins = pe.transpose(bank[b][:, c:c + P], gxn[:, 2 * pair + v, k * P:(k + 1) * P], ident[:])
                ins.then_inc(S.nT, 1)

            def conv_mm(g, k_):
                i = NC * g + k_
                c0 = DI + H + CONV_ORDER[k_] * P
                pe.wait_ge(S.nlo, 2 * g + 2)
                b = piece_bank(g, f"c{k_}")
                reuse(b, S.tap, (TAPS - 1) * (i + 1))
                for k in range(KD):
                    ins = product(bank[b][:], (wih[:, k, c0:c0 + P], wil[:, k, c0:c0 + P]),
                                  (nTh[:, k, :], nTl[:, k, :]), k == 0, k == KD - 1)
                ins.then_inc(S.conv, 1)

            def z_mm(g, j, half):
                i = G * g + j
                pe.wait_ge(S.nlo, 2 * g + 2)
                cols = slice(j * P, (j + 1) * P)
                b, w = piece_bank(g, f"z{half}{j}"), [slice(0, ZC), slice(ZC, ZC + D)][half]
                reuse(b, *[(S.z0_out, i + 1), (S.zs, i + 1)][half])
                for k in range(KD):
                    lhs = (nTh[:, k, cols], nTl[:, k, cols])
                    ins = product(bank[b][:, 0:ZC if half == 0 else D], lhs, (wih[:, k, w], wil[:, k, w]),
                                  k == 0, k == KD - 1)
                ins.then_inc([S.z0, S.z1][half], 1)

            def z0_mm(g, j):
                z_mm(g, j, 0)

            def z1_mm(g, j):
                z_mm(g, j, 1)

            def segments(t):
                pe.wait_ge(S.decay, 2 * (t + 1))
                for half in range(2):
                    reuse(half, S.exp, 2 * t + half + 1)
                    hs = slice(4 * half, 4 * half + 4)
                    pe.matmul(bank[half][:], below_r[:], rh[:, hs, :].rearrange("p h n -> p (h n)"), start=True, stop=False)
                    ins = pe.matmul(bank[half][:], below_r[:], rl[:, hs, :].rearrange("p h n -> p (h n)"), start=False, stop=True)
                ins.then_inc(S.seg, 1)

            def decay_sum(t):
                g, j = divmod(t, G)
                pe.wait_ge(S.dA, 2 * (g + 1))
                reuse(3, S.edec, t + 1)
                pe.matmul(bank[3][:, P:P + H], below[:] if t % 2 == 0 else upto[:], dA[:, g % 2, j, :], start=True,
                          stop=True).then_inc(S.dec, 1)

            def c_b(t):
                g, j = divmod(t, G)
                cols = slice(j * P, (j + 1) * P)
                pe.wait_ge(S.xc, NC * (g + 1))
                if t % 2 == 0:
                    reuse(3, S.btok, t // 2 + 1)
                    pe.transpose(bank[3][:, 256:256 + N], BT[:, g % 2, cols], ident[0:N, 0:N])
                else:
                    reuse(3, S.cbm, t + 1)
                pe.matmul(bank[3][:, 0:P], BT[:, g % 2, cols], CT[:, g % 2, cols], start=True, stop=True).then_inc(S.misc, 1)

            def x_tokens(t):
                g, j = divmod(t, G)
                pe.wait_ge(S.xc, NC * (g + 1))
                if t:
                    pe.wait_ge(S.dtx, t)
                reuse(2, S.xD, t + 1)
                for c in range(KI):
                    ins = pe.transpose(bank[2][:, c * P:(c + 1) * P], xc[:, g % 2, c, j * P:(j + 1) * P], ident[:])
                ins.then_inc(S.xtok, 1)

            def y_turn(t):
                pe.wait_ge(S.yz, t + 1)
                reuse(turned_bank(t), S.ylo, t + 1)
                for c in range(KI):
                    ins = pe.transpose(bank[turned_bank(t)][:, c * P:(c + 1) * P], yz[:, t % 2, c * P:(c + 1) * P], ident[:])
                ins.then_inc(S.yT, 1)

            def y_sum(t):
                pe.wait_ge(S.M, 2 * (t + 1))
                pe.wait_ge(S.dtx, t + 1)
                reuse(4, S.y, t + 1)
                for h in range(H):
                    ins = pe.matmul(bank[4][:, h * HD:(h + 1) * HD], M[:, t % 2, h, :], dtx[:, t % 2, h * HD:(h + 1) * HD],
                                    start=True, stop=True)
                ins.then_inc(S.y_mm, 1)

            def carry(t):
                g, j = divmod(t, G)
                if t % 2 == 0:
                    pe.wait_ge(S.dtxe, t // 2 + 1)
                    pe.wait_ge(S.btok, t // 2 + 1)
                    reuse(7, S.state, t // 2 + 1)
                    pe.matmul(bank[7][0:N, :], Btok[:], dtxe, start=True, stop=True).then_inc(S.carry, 1)
                else:
                    pe.wait_ge(S.state, t // 2 + 1)
                    reuse(7, S.off, t // 2 + 1)
                    pe.matmul(bank[7][:], CT[:, g % 2, j * P:(j + 1) * P], state[:], start=True, stop=True).then_inc(S.off_mm, 1)

            def o_mm(t):
                pe.wait_ge(S.ylo, t + 1)
                b = out_bank(t)
                reuse(b, S.added, t + 1)
                for c in range(KI):
                    ins = product(bank[b][:, 0:D], (yTh[:, c, :], yTl[:, c, :]), (woh[:, c, :], wol[:, c, :]), c == 0, c == KI - 1)
                ins.then_inc(S.o, 1)

            def first_group(t, j):
                if t == T - 4 and j == 5:
                    pe.wait_ge(const_done, 9)
                    pe.wait_ge(late_split, 2 * (len(chunks) - LATE))
                    pe.wait_ge(FFN[0].xlo, T - 2)
                    n_turn(0, 0)
                if t == T - 4 and j == 7:
                    n_turn(0, 1)
                if t == T - 3 and 4 <= j < 8:
                    pe.wait_ge(FFN[0].xlo, T - 1)
                    z_mm(0, j - 4, 0)
                if t == T - 2 and j == 5:
                    pe.wait_ge(FFN[0].xlo, T)
                    conv_mm(0, 0)
                if t == T - 1 and j in (1, 5, 7):
                    conv_mm(0, j // 3 + 1)

            def last_tile(t, j):
                if t == 0 and j == 2:
                    y_turn(T - 1)
                if t == 0 and j == 4:
                    o_mm(T - 1)

            pe.wait_ge(const_done, 8)
            x_turn(FFN[0], 0, 0)
            gate_up(FFN[0], 0, 0, 0, 0, SH)
            h_turn(FFN[0], 0, 0)
            ffn(FFN[0], first_group)

            segments(0)
            decay_sum(0)
            conv_mm(0, 4)
            for j in range(G):
                z1_mm(0, j)
            for n in range(-3, T + 6):
                g, j = divmod(n, G)
                if j == 0:
                    of_tile(decay_sum, n, first=1)
                    of_group(n_turn, g + 1, 1)
                    of_tile(segments, n, first=1)
                    of_tile(o_mm, n - 3, last=T - 2)
                    if n == T:
                        reuse(5, FFN[1].xlo, 1)
                        x_turn(FFN[1], 0, 0)
                    of_tile(y_sum, n - 1)
                    of_tile(carry, n - 1)
                    if n == T:
                        reuse(1, FFN[1].hidden, 1)
                        gate_up(FFN[1], 0, 0, 0, 0, SH)
                    of_tile(y_turn, n - 2, last=T - 2)
                    of_tile(x_tokens, n + 1)
                    of_tile(c_b, n)
                    of_group(z0_mm, g + 1, 0)
                elif j == 1:
                    of_group(z0_mm, g + 1, 1)
                    of_tile(c_b, n)
                    of_tile(segments, n, first=1)
                    of_tile(o_mm, n - 3, last=T - 2)
                    of_group(z0_mm, g + 1, 2)
                    of_tile(decay_sum, n, first=1)
                    of_tile(y_turn, n - 2, last=T - 2)
                    of_group(z0_mm, g + 1, 3)
                    of_tile(y_sum, n - 1)
                    of_group(conv_mm, g + 1, 0)
                    of_tile(x_tokens, n + 1)
                    of_tile(c_b, n + 1)
                    of_group(conv_mm, g + 1, 1)
                    of_tile(carry, n - 1)
                    of_tile(segments, n + 1, first=1)
                elif j == 2:
                    of_tile(o_mm, n - 3, last=T - 2)
                    of_tile(decay_sum, n, first=1)
                    of_group(z1_mm, g + 1, 0)
                    of_tile(y_turn, n - 2, last=T - 2)
                    of_tile(y_sum, n - 1)
                    of_tile(carry, n - 1)
                    of_group(conv_mm, g + 1, 2)
                    of_tile(x_tokens, n + 1)
                else:
                    of_group(conv_mm, g + 1, 3)
                    of_tile(segments, n, first=1)
                    of_tile(decay_sum, n, first=1)
                    of_tile(o_mm, n - 3, last=T - 2)
                    of_group(conv_mm, g + 1, 4)
                    of_tile(y_sum, n - 1)
                    of_tile(y_turn, n - 2, last=T - 2)
                    of_group(z1_mm, g + 1, 1)
                    of_tile(c_b, n)
                    of_tile(carry, n - 1)
                    of_group(z1_mm, g + 1, 2)
                    of_group(z1_mm, g + 1, 3)
                    of_group(n_turn, g + 2, 0)
                    of_tile(x_tokens, n + 1)

            reuse(4, FFN[1].hlo, 1)
            h_turn(FFN[1], 0, 0)
            for b in (0, 2, 3, 5):
                reuse(b, None, None)
            ffn(FFN[1], last_tile)


def kernel(L0_attn_u, L0_attn_W_in, L0_attn_conv_w, L0_attn_conv_b, L0_attn_dt_bias, L0_attn_A_log,
           L0_attn_D_param, L0_attn_norm_w, L0_attn_W_out, L0_ffn_router_w, L0_ffn_gate_up_w, L0_ffn_down_w,
           L0_ffn_shared_gate_w, L0_ffn_shared_up_w, L0_ffn_shared_down_w):
    import numpy as np
    import concourse.bacc as bacc
    from concourse.bass_utils import run_bass_kernel_spmd

    u = np.asarray(L0_attn_u)
    w_in = np.asarray(L0_attn_W_in)
    half = DI // 2
    arrays = {
        "u": u.reshape(-1, D),
        "wg_up": L0_ffn_gate_up_w,
        "w_down": L0_ffn_down_w,
        "w_sh_gate": L0_ffn_shared_gate_w,
        "w_sh_up": L0_ffn_shared_up_w,
        "w_sh_down": L0_ffn_shared_down_w,
        "w_router": L0_ffn_router_w,
        "w_in_t": np.concatenate([w_in[:half], w_in[-H:], w_in[half:-H]], axis=0).T,
        "w_out_t": np.asarray(L0_attn_W_out).T,
        "conv_w": np.asarray(L0_attn_conv_w).reshape(NC, P, TAPS).transpose(1, 0, 2),
        "conv_b": np.asarray(L0_attn_conv_b).reshape(NC, P).T,
        "dt_bias": L0_attn_dt_bias,
        "a_log": L0_attn_A_log,
        "d_param": L0_attn_D_param,
        "norm_w": np.asarray(L0_attn_norm_w).reshape(KI, P).T,
    }
    nc = bacc.Bacc("TRN2", target_bir_lowering=False, num_devices=1)
    feeds, args = {}, []
    for name, a in arrays.items():
        a = np.ascontiguousarray(a)
        feeds[f"{name}_dram"] = a
        args.append(nc.dram_tensor(f"{name}_dram", a.shape, mybir.dt.from_np(a.dtype), kind="ExternalInput").ap())
    args.append(nc.dram_tensor("out_dram", (u.size // D, D), F32, kind="ExternalOutput").ap())
    macaron_kernel(nc, *args)
    r = run_bass_kernel_spmd(nc, [feeds], core_ids=[0])
    return r.results[0]["out_dram"].reshape(u.shape)
```
